# Optimizing a Trainium2 kernel written in Bass

```python
import numpy as np
import jax
import jax.numpy as jnp

def _softmax(x, axis=-1):
    return jax.nn.softmax(x, axis=axis)

def _gelu(x):
    return jax.nn.gelu(x, approximate=True)

def _silu(x):
    return jax.nn.silu(x)

def _sigmoid(x):
    return jax.nn.sigmoid(x)

def _layernorm(x, axis=-1, eps=1e-05):
    m = jnp.mean(x, axis=axis, keepdims=True)
    v = jnp.var(x, axis=axis, keepdims=True)
    return (x - m) / jnp.sqrt(v + eps)

def _scatter_add(tgt, idx, src, axis=0):
    return tgt.at[idx].add(src)

def _segment_sum(src, seg, n):
    return jax.ops.segment_sum(src, seg, n)
kernel_name = 'mk_adj_ffn_d1_adj_r2_6ab273'

def setup_inputs(seed: int=0):
    np.random.seed(seed)
    _w = jnp.asarray

    def _rec_inputs():
        import jax
        import jax.numpy as jnp
        _gk = jax.random.key(seed)
        x = -0.0002928 + 1 * jax.random.normal(jax.random.fold_in(_gk, 1), (1354, 256), jnp.float32)
        _w = (1.0 + jnp.arange(1354, dtype=jnp.float32)) ** (-0.5)
        _w = _w / _w.mean()
        _pij = jnp.clip(0.0118168 * _w[:, None] * _w[None, :], 0.0, 1.0)
        _a = jax.random.uniform(jax.random.fold_in(_gk, 2), (1354, 1354)) < _pij
        _a = jnp.logical_or(_a, jnp.swapaxes(_a, -1, -2))
        _a = jnp.logical_or(_a, jnp.eye(1354, dtype=bool))
        _af = _a.astype(jnp.float32)
        _af = _af * jax.random.uniform(jax.random.fold_in(_gk, 3), (1354, 1354), jnp.float32, 0.05, 5.41998)
        adj = _af
        return (x, adj)
    x, adj = _rec_inputs()

    def _L0_gnn_setup():
        import jax, jax.numpy as jnp
        import numpy as np
        N = 4096
        D = 256
        key = jax.random.key(seed)
        ks = jax.random.split(key, 6)
        s = 1.0 / np.sqrt(D)
        return {'x': jax.random.normal(ks[0], (N, D), jnp.float32), 'spatial_encoding': jax.random.normal(ks[1], (N, N), jnp.float32), 'edge_encoding': jax.random.normal(ks[2], (N, N), jnp.float32), 'Wq': jax.random.normal(ks[3], (D, D), jnp.float32) * s, 'bq': jnp.zeros((D,), jnp.float32), 'Wk': jax.random.normal(ks[4], (D, D), jnp.float32) * s, 'bk': jnp.zeros((D,), jnp.float32), 'Wv': jax.random.normal(ks[5], (D, D), jnp.float32) * s, 'bv': jnp.zeros((D,), jnp.float32)}
    _L0_gnn_all = _L0_gnn_setup()
    _L0_gnn_in = {k: v for k, v in _L0_gnn_all.items() if k in ('Wq', 'bq', 'Wk', 'bk', 'Wv', 'bv')}
    del _L0_gnn_all

    def _L0_ffn_setup():
        import jax, jax.numpy as jnp
        import numpy as np
        K = 2
        EPS = 1e-06

        def _layernorm(x, gamma, beta):
            mu = jnp.mean(x, axis=-1, keepdims=True)
            var = jnp.mean(jnp.square(x - mu), axis=-1, keepdims=True)
            return (x - mu) * jax.lax.rsqrt(var + EPS) * gamma + beta
        key = jax.random.key(seed)
        ks = jax.random.split(key, 5)
        B, S, D, F, E = (8, 1024, 256, 1024, 8)
        x = jax.random.normal(ks[0], (B, S, D), dtype=jnp.float32)
        router_w = jax.random.normal(ks[1], (D, E), dtype=jnp.float32) * 0.02
        w1 = jax.random.normal(ks[2], (E, D, F), dtype=jnp.float32) * 0.02
        b1 = jnp.zeros((E, F), dtype=jnp.float32)
        w2 = jax.random.normal(ks[3], (E, F, D), dtype=jnp.float32) * 0.02
        b2 = jnp.zeros((E, D), dtype=jnp.float32)
        gamma = jnp.ones((E, D), dtype=jnp.float32)
        beta = jnp.zeros((E, D), dtype=jnp.float32)
        return {'x': x, 'router_w': router_w, 'w1': w1, 'b1': b1, 'w2': w2, 'b2': b2, 'gamma': gamma, 'beta': beta}
    _L0_ffn_all = _L0_ffn_setup()
    _L0_ffn_in = {k: v for k, v in _L0_ffn_all.items() if k in ('router_w', 'w1', 'b1', 'w2', 'b2', 'gamma', 'beta')}
    del _L0_ffn_all
    return {'x': x, 'adj': adj, 'L0_gnn_Wq': _L0_gnn_in['Wq'], 'L0_gnn_bq': _L0_gnn_in['bq'], 'L0_gnn_Wk': _L0_gnn_in['Wk'], 'L0_gnn_bk': _L0_gnn_in['bk'], 'L0_gnn_Wv': _L0_gnn_in['Wv'], 'L0_gnn_bv': _L0_gnn_in['bv'], 'L0_ffn_router_w': _L0_ffn_in['router_w'], 'L0_ffn_w1': _L0_ffn_in['w1'], 'L0_ffn_b1': _L0_ffn_in['b1'], 'L0_ffn_w2': _L0_ffn_in['w2'], 'L0_ffn_b2': _L0_ffn_in['b2'], 'L0_ffn_gamma': _L0_ffn_in['gamma'], 'L0_ffn_beta': _L0_ffn_in['beta']}

def reference(x, adj, L0_gnn_Wq, L0_gnn_bq, L0_gnn_Wk, L0_gnn_bk, L0_gnn_Wv, L0_gnn_bv, L0_ffn_router_w, L0_ffn_w1, L0_ffn_b1, L0_ffn_w2, L0_ffn_b2, L0_ffn_gamma, L0_ffn_beta):
    import jax
    import jax.numpy as jnp

    def _L0_gnn_ref(x, spatial_encoding, edge_encoding, Wq, bq, Wk, bk, Wv, bv):
        import jax, jax.numpy as jnp
        import numpy as np
        N = 4096
        D = 256
        q = x @ Wq.T + bq
        k = x @ Wk.T + bk
        v = x @ Wv.T + bv
        scale = 1.0 / jnp.sqrt(jnp.asarray(q.shape[-1], q.dtype))
        a = q @ k.T * scale + spatial_encoding + edge_encoding
        attn = jax.nn.softmax(a, axis=-1)
        return attn @ v

    def _L0_ffn_ref(x, router_w, w1, b1, w2, b2, gamma, beta):
        import jax, jax.numpy as jnp
        import numpy as np
        K = 2
        EPS = 1e-06

        def _layernorm(x, gamma, beta):
            mu = jnp.mean(x, axis=-1, keepdims=True)
            var = jnp.mean(jnp.square(x - mu), axis=-1, keepdims=True)
            return (x - mu) * jax.lax.rsqrt(var + EPS) * gamma + beta
        B, S, D = x.shape
        E = w1.shape[0]
        xf = x.reshape(-1, D)
        logits = xf @ router_w
        gate_vals, idx = jax.lax.top_k(logits, K)
        gates = jax.nn.softmax(gate_vals, axis=-1)
        out = jnp.zeros_like(xf)
        for e in range(E):
            h = jax.nn.relu(xf @ w1[e] + b1[e]) @ w2[e] + b2[e]
            y = _layernorm(xf + h, gamma[e], beta[e])
            w = jnp.sum(jnp.where(idx == e, gates, 0.0), axis=-1)
            out = out + w[:, None] * y
        return out.reshape(B, S, D)
    x = x + _L0_gnn_ref(_layernorm(x, axis=-1), adj, adj, L0_gnn_Wq, L0_gnn_bq, L0_gnn_Wk, L0_gnn_bk, L0_gnn_Wv, L0_gnn_bv)
    x = x + _L0_ffn_ref(_layernorm(x, axis=-1)[None], L0_ffn_router_w, L0_ffn_w1, L0_ffn_b1, L0_ffn_w2, L0_ffn_b2, L0_ffn_gamma, L0_ffn_beta)[0]
    return x

_drawn_inputs = setup_inputs


def setup_inputs(seed=0):
    import zlib

    import numpy as np

    out = dict(_drawn_inputs(seed))
    spreads = {'L0_gnn_bq': (0.0, 0.1),
     'L0_gnn_bk': (0.0, 0.8),
     'L0_gnn_bv': (0.0, 0.1),
     'L0_ffn_b1': (0.0, 0.519),
     'L0_ffn_b2': (0.0, 0.1),
     'L0_ffn_gamma': (1.0, 0.2),
     'L0_ffn_beta': (0.0, 0.1)}
    factors = {}
    for name, (base, spread) in spreads.items():
        noise = np.random.default_rng([zlib.crc32(name.encode()), seed]).standard_normal(out[name].shape)
        drawn = base * np.exp(spread * noise) if base else spread * noise
        out[name] = jnp.asarray(drawn.astype(out[name].dtype))
    for name, factor in factors.items():
        out[name] = (out[name] * factor).astype(out[name].dtype)
    return out
```

```python
from contextlib import ExitStack

import numpy as np

import concourse.bass as bass
from concourse import mybir

F32 = mybir.dt.float32
I32 = mybir.dt.int32
U32 = mybir.dt.uint32
ALU = mybir.AluOpType
ACT = mybir.ActivationFunctionType
AX = mybir.AxisListType

P = 128
BANK = 512
LN_EPS = 1e-5
EXPERT_EPS = 1e-6
LEAST = -3.0e38


def block_kernel(nc, x, adj, wqT, wkT, wvT, bias_cols, bv, router_w, w1, b1, w2, norm_rows, out):
    N, D = x.shape
    E, _, F = w1.shape
    K = 2
    T = (N + P - 1) // P
    TAIL = N - (T - 1) * P
    NP = T * P
    DC = D // P
    FC = F // P
    HB = F // BANK
    SLOT_TILES = (K * N + E * (P - 1)) // P
    PAIRS = K * N
    KEY_BANKS = [(b, min(BANK, N - b)) for b in range(0, N, BANK)]
    CHUNKS_PER_BANK = BANK // P
    QK_SCALE = float(D) ** -0.5 / 2

    xf_dram = nc.dram_tensor("xf_rows", (N, D), F32, kind="Internal").ap()
    pair_dram = nc.dram_tensor("pair_rows", (PAIRS + SLOT_TILES * P, D), F32, kind="Internal").ap()

    with ExitStack() as ctx:
        def sb(name, shape, dt=F32):
            return ctx.enter_context(nc.sbuf_tensor(name, shape, dt))

        def sem(name):
            return ctx.enter_context(nc.semaphore(name))

        psum = ctx.enter_context(nc.psum_tensor("psum", [P, 8, BANK], F32))

        w1_sb = sb("w1_sb", [P, E, DC, F])
        w2_sb = sb("w2_sb", [P, E, FC, D])
        x_res = sb("x_res", [P, T, D])
        qkT = sb("qkT", [P, 2, DC, NP])
        qT, kT = qkT[:, 0], qkT[:, 1]
        v_sb = sb("v_sb", [P, T, D])
        adj_sb = sb("adj_sb", [P, 2, N])
        prob = sb("prob", [P, N])
        probT = sb("probT", [P, T, P])
        wqkv = sb("wqkv", [P, 3, DC, D])
        q_now = sb("q_now", [P, DC, P])
        xf_now = sb("xf_now", [P, D])
        xfT = sb("xfT", [P, DC, P])
        bias_qk = sb("bias_qk", [P, 2, DC])
        bv_rows = sb("bv_rows", [P, D])
        router = sb("router", [P, DC, E])
        stats = sb("stats", [P, 6])
        mean = sb("mean", [P, T])
        rstd = sb("rstd", [P, T])
        minus_half = sb("minus_half", [P, T])
        row_max = sb("row_max", [P, 1])
        neg_max = sb("neg_max", [P, 1])
        row_sum = sb("row_sum", [P, 1])
        row_inv = sb("row_inv", [P, 1])
        moments2 = sb("moments2", [P, 2])
        var2 = sb("var2", [P, 1])
        rstd2 = sb("rstd2", [P, 1])
        expert_no = sb("expert_no", [P, E])
        var_eps = sb("var_eps", [P, T])
        logit = sb("logit", [P, T, E])
        stats2 = sb("stats2", [P, 6])
        held = sb("held", [P, 2])
        ident = sb("ident", [P, P])
        col = sb("col", [P, P])
        part = sb("part", [P, 1])
        pair_no = sb("pair_no", [P, T, K])
        spare = sb("spare", [P, SLOT_TILES])
        tile_edges = sb("tile_edges", [P, T])
        spare_col = sb("spare_col", [P, SLOT_TILES])
        order = sb("order", [P, E, E])
        lower = sb("lower", [P, E, E])
        gates = sb("gates", [P, T, K])
        gate_tmp = sb("gate_tmp", [P, 3, T])
        block_start = sb("block_start", [P, E])
        tiles_of = sb("tiles_of", [P, E])
        tile_expert = sb("tile_expert", [P, SLOT_TILES])
        tile_expert_i = sb("tile_expert_i", [P, SLOT_TILES], I32)
        expert_hot = sb("expert_hot", [E, SLOT_TILES])
        slot_pair = sb("slot_pair", [P, SLOT_TILES], I32)
        slot_token = sb("slot_token", [P, SLOT_TILES], I32)
        pair_now = sb("pair_now", [P, 1], I32)
        token_now = sb("token_now", [P, 1], I32)

        xn = adj_sb[:, 1, 0:D]
        xnT = probT[:, 0:2 * DC, :].rearrange("p (u c) n -> p u c n", u=2)
        w_flat = wqkv[:, :, :, :].rearrange("p w c o -> p (w c o)")
        b1_rows = w_flat[0:E, 0:F]
        before = w_flat[:, F:F + P]
        ones = w_flat[:, F + P:F + 2 * P]
        assert SLOT_TILES * FC <= D
        b1_tiles = bv_rows[:, 0:SLOT_TILES * FC].rearrange("p (i c) -> p i c", c=FC)
        qk_flat = qkT[:, :, :, :].rearrange("p w c n -> p (w c n)")
        used = [0]

        def carve(*shape):
            n = int(np.prod(shape))
            used[0] += n
            assert used[0] <= 2 * DC * NP
            flat = qk_flat[:, used[0] - n:used[0]]
            if len(shape) == 1:
                return flat
            if len(shape) == 2:
                return flat.rearrange("p (a b) -> p a b", a=shape[0])
            return flat.rearrange("p (a b c) -> p a b c", a=shape[0], b=shape[1])

        row_hot = carve(T * K, P)
        blk_hot = carve(T * K, SLOT_TILES)
        hot = carve(T, K, E)
        best = carve(T, K)
        rest = carve(T, E)
        is_best = carve(T, E)
        where_best = carve(T)
        member = carve(T, E)
        earlier = carve(T, E)
        slot_base = carve(T, E)
        slot_pick = carve(T * K, E)
        slot_f = carve(T * K)
        slot_i = carve(T * K).bitcast(I32)
        slot_row_i = carve(T * K).bitcast(I32)
        slot_blk_i = carve(T * K).bitcast(I32)
        slot_row = carve(T * K)
        slot_blk = carve(T * K)
        tile_cmp = carve(E, T)
        start_cmp = carve(E, E)
        expert_cmp = carve(SLOT_TILES, E - 1)
        slot_tmp = carve(SLOT_TILES)
        slot_tok_i = carve(SLOT_TILES).bitcast(I32)
        vflat = v_sb[:, :, :].rearrange("p t d -> p (t d)")
        x_slot = adj_sb[:, 0, 0:D]
        xT_slot = adj_sb[:, 0, D:2 * D].rearrange("p (c n) -> p c n", c=DC)
        h_sb = vflat[:, 0:F]
        hT_sb = vflat[:, F:2 * F].rearrange("p (c n) -> p c n", c=FC)
        NORM_RING, XB_RING = 4, 4
        norm_sb = qk_flat[:, 0:NORM_RING * 3 * D]\
            .rearrange("p (r a d) -> p r a d", r=NORM_RING, a=3)
        xb_slot = adj_sb[:, 1, 0:XB_RING * D].rearrange("p (r d) -> p r d", r=XB_RING)
        y_sum = prob[:, 0:D]
        y_mid = prob[:, D:2 * D]
        y_out = prob[:, 2 * D:3 * D]
        pair_sb = w1_sb[:, :, :, :].rearrange("p e c f -> p (e c f)")[:, 0:T * K * D]\
            .rearrange("p (t k d) -> p t k d", t=T, k=K)

        x_loaded = sem("x_loaded")
        w_loaded = sem("w_loaded")
        small_loaded = sem("small_loaded")
        adj_loaded = [sem("adj_loaded_even"), sem("adj_loaded_odd")]
        b1_loaded = sem("b1_loaded")
        expert_loaded = sem("expert_loaded")
        xf_stored = sem("xf_stored")
        norm_loaded = sem("norm_loaded")
        x_gathered = sem("x_gathered")
        pair_stored = sem("pair_stored")
        pair_loaded = sem("pair_loaded")
        out_stored = sem("out_stored")
        pad_zeroed = sem("pad_zeroed")
        iotas = sem("iotas")
        consts = sem("consts")
        moments_ready = sem("moments_ready")
        rstd_ready = sem("rstd_ready")
        xn_ready = sem("xn_ready")
        bv_added = sem("bv_added")
        xnT_done = sem("xnT_done")
        xnT_ready = sem("xnT_ready")
        qkv_done = sem("qkv_done")
        qkv_ready = sem("qkv_ready")
        q_copied = sem("q_copied")
        s_done = sem("s_done")
        max_ready = sem("max_ready")
        p_ready = sem("p_ready")
        pT_done = sem("pT_done")
        pT_by_act = sem("pT_by_act")
        pT_by_dve = sem("pT_by_dve")
        pv_done = sem("pv_done")
        moments2_ready = sem("moments2_ready")
        rstd2_ready = sem("rstd2_ready")
        xf_ready = sem("xf_ready")
        xfT_done = sem("xfT_done")
        xfT_ready = sem("xfT_ready")
        logits_done = sem("logits_done")
        logit_ready = sem("logit_ready")
        gap_ready = sem("gap_ready")
        gap_exp = sem("gap_exp")
        member_ready = sem("member_ready")
        rank_done = sem("rank_done")
        hot_ready = sem("hot_ready")
        expert_hot_ready = sem("expert_hot_ready")
        b1_done = sem("b1_done")
        b1_ready = sem("b1_ready")
        slots_done = sem("slots_done")
        slots_ready = sem("slots_ready")
        xb_ready = sem("xb_ready")
        xT_done = sem("xT_done")
        xT_ready = sem("xT_ready")
        h_done = sem("h_done")
        h_copied = sem("h_copied")
        hT_done = sem("hT_done")
        hT_ready = sem("hT_ready")
        z_done = sem("z_done")
        z_read = sem("z_read")
        y_moments = sem("y_moments")
        y_rstd = sem("y_rstd")
        y_ready = sem("y_ready")
        index_ready = sem("index_ready")
        out_ready = sem("out_ready")
        xb_read = sem("xb_read")
        token_ready = sem("token_ready")
        inv_ready = sem("inv_ready")
        gate_ready = sem("gate_ready")
        spare_ready = sem("spare_ready")
        dve_setup = sem("dve_setup")
        moment_step = sem("moment_step")
        softmax_step = sem("softmax_step")
        finish_step = sem("finish_step")
        route_step = sem("route_step")
        y_step = sem("y_step")
        out_step = sem("out_step")
        pool_step = sem("pool_step")

        block = ctx.enter_context(nc.Block())

        @block.sync
        def _(sp):
            sp.wait_ge(pad_zeroed, 1)
            sp.dma_start(x_res[:, 0, :], x[0:P, :]).then_inc(x_loaded, 16)
            sp.dma_start(wqkv[:, 1], wkT.rearrange("(c p) o -> p c o", p=P)).then_inc(w_loaded, 16)
            sp.dma_start(wqkv[:, 0], wqT.rearrange("(c p) o -> p c o", p=P)).then_inc(w_loaded, 16)
            sp.dma_start(wqkv[:, 2], wvT.rearrange("(c p) o -> p c o", p=P)).then_inc(w_loaded, 16)
            sp.dma_start(x_res[:, 1:T - 1, :], x[P:(T - 1) * P, :].rearrange("(t p) d -> p t d", p=P))\
                .then_inc(x_loaded, 16)
            sp.dma_start(x_res[0:TAIL, T - 1, :], x[(T - 1) * P:N, :]).then_inc(x_loaded, 16)
            sp.dma_start(bias_qk[:], bias_cols).then_inc(small_loaded, 16)
            sp.dma_start(bv_rows[:, :], bv.rearrange("(a d) -> a d", a=1).broadcast_to((P, D)))\
                .then_inc(small_loaded, 16)
            sp.dma_start(router[:, :, :], router_w.rearrange("(c p) e -> p c e", p=P)).then_inc(small_loaded, 16)
            sp.dma_start(adj_sb[:, 0, :], adj[0:P, :]).then_inc(adj_loaded[0], 16)
            sp.wait_ge(qkv_done, T)
            sp.dma_start(b1_rows, b1).then_inc(b1_loaded, 16)
            sp.wait_ge(xnT_done, T)
            sp.dma_start(adj_sb[:, 1, :], adj[P:2 * P, :]).then_inc(adj_loaded[1], 16)

            def load_expert(e):
                sp.dma_start(w1_sb[:, bass.ds(e, 1)], w1[bass.ds(e, 1)].rearrange("a (c p) f -> p a c f", p=P))\
                    .then_inc(expert_loaded, 16)
                sp.dma_start(w2_sb[:, bass.ds(e, 1)], w2[bass.ds(e, 1)].rearrange("a (c p) d -> p a c d", p=P))\
                    .then_inc(expert_loaded, 16)

            def store_xf(t, rows):
                sp.wait_ge(xf_ready, t + 1)
                sp.dma_start(xf_dram[bass.ds(t * P, rows), :], xf_now[0:rows, :]).then_inc(xf_stored, 16)

            def load_adj(t, u, rows):
                sp.wait_ge(p_ready, t - 1)
                sp.dma_start(adj_sb[0:rows, u, :], adj[bass.ds(t * P, rows), :]).then_inc(adj_loaded[u], 16)

            with sp.Fori(0, E - 1, 2) as i:
                for u in range(2):
                    load_adj(i + u + 2, u, P)
                    load_expert(i + u)
                    store_xf(i + u, P)
            assert E == T - 3
            load_adj(T - 1, (T - 1) % 2, TAIL)
            for t in range(E, T):
                store_xf(t, TAIL if t == T - 1 else P)

            sp.wait_ge(pair_stored, 16 * SLOT_TILES)
            groups = [(0, 4), (4, 8), (8, T - 1)]
            for a, b in groups:
                sp.dma_start(pair_sb[:, a:b], pair_dram[a * P * K:b * P * K, :]
                             .rearrange("(t p k) d -> p t k d", p=P, k=K)).then_inc(pair_loaded, 16)
            sp.dma_start(pair_sb[0:TAIL, T - 1], pair_dram[(T - 1) * P * K:PAIRS, :]
                         .rearrange("(p k) d -> p k d", k=K)).then_inc(pair_loaded, 16)
            for a, b in groups:
                sp.wait_ge(out_ready, b)
                sp.dma_start(out[a * P:b * P, :].rearrange("(t p) d -> p t d", p=P), x_res[:, a:b, :])\
                    .then_inc(out_stored, 16)
            sp.wait_ge(out_ready, T)
            sp.dma_start(out[(T - 1) * P:N, :], x_res[0:TAIL, T - 1, :]).then_inc(out_stored, 16)
            sp.wait_ge(out_stored, 16 * (len(groups) + 1))

        @block.tensor
        def _(pe):
            pe.wait_ge(consts, 1)

            def turn_xn(t):
                pe.wait_ge(xn_ready, t + 1)
                for c in range(DC):
                    m = pe.transpose(psum[:, 0, c * P:(c + 1) * P], xn[:, c * P:(c + 1) * P], ident[:])
                m.then_inc(xnT_done, 1)

            def project(t, u):
                pe.wait_ge(xnT_ready, t + 1)
                for w in (1, 0):
                    for o in range(DC):
                        for c in range(DC):
                            m = pe.matmul(psum[:, 1 + u, (w * DC + o) * P:(w * DC + o + 1) * P],
                                          wqkv[:, w, c, o * P:(o + 1) * P], xnT[:, u, c, :],
                                          start=(c == 0), stop=(c == DC - 1))
                for c in range(DC):
                    m = pe.matmul(psum[:, 3 + u, 0:D], xnT[:, u, c, :], wqkv[:, 2, c, :],
                                  start=(c == 0), stop=(c == DC - 1))
                m.then_inc(qkv_done, 1)

            turn_xn(0)
            pe.wait_ge(w_loaded, 48)
            pe.wait_ge(xnT_ready, 1)
            turn_xn(1)
            project(0, 0)
            pe.wait_ge(xnT_ready, 2)
            turn_xn(2)
            project(1, 1)
            with pe.Fori(2, T - 2, 2) as i:
                for u in range(2):
                    t = i + u
                    pe.wait_ge(xnT_ready, t + 1)
                    turn_xn(t + 1)
                    pe.wait_ge(qkv_ready, t - 1)
                    project(t, u)
            pe.wait_ge(qkv_ready, T - 2)
            project(T - 1, 0)

            def scores(t):
                pe.wait_ge(q_copied, t + 1)
                for b, (k0, kn) in enumerate(KEY_BANKS):
                    for c in range(DC):
                        m = pe.matmul(psum[:, b, 0:kn], q_now[:, c, :], kT[:, c, k0:k0 + kn],
                                      start=(c == 0), stop=(c == DC - 1))
                m.then_inc(s_done, 1)

            def turn_probs(t):
                pe.wait_ge(p_ready, t + 1)
                for j in range(T):
                    rows = min(P, N - j * P)
                    a = j % CHUNKS_PER_BANK * P
                    m = pe.transpose(psum[0:rows, 3 + j // CHUNKS_PER_BANK, a:a + P],
                                     prob[:, j * P:j * P + rows], ident[:])
                m.then_inc(pT_done, 1)

            def weigh_values(t):
                pe.wait_ge(pT_by_act, t + 1)
                pe.wait_ge(pT_by_dve, t + 1)
                for j in range(T):
                    rows = min(P, N - j * P)
                    m = pe.matmul(psum[:, 6, 0:D], probT[0:rows, j, :], v_sb[0:rows, j, :],
                                  start=(j == 0), stop=(j == T - 1))
                m.then_inc(pv_done, 1)

            def turn_xf(t):
                pe.wait_ge(xf_ready, t + 1)
                for c in range(DC):
                    m = pe.transpose(psum[:, 7, c * P:(c + 1) * P], xf_now[:, c * P:(c + 1) * P], ident[:])
                m.then_inc(xfT_done, 1)

            def logits(t):
                pe.wait_ge(xfT_ready, t + 1)
                for c in range(DC):
                    m = pe.matmul(psum[:, 7, D:D + E], xfT[:, c, :], router[:, c, :],
                                  start=(c == 0), stop=(c == DC - 1))
                m.then_inc(logits_done, 1)

            pe.wait_ge(qkv_ready, T)
            pe.wait_ge(small_loaded, 48)
            scores(0)
            turn_probs(0)
            scores(1)
            weigh_values(0)
            turn_probs(1)
            scores(2)
            turn_xf(0)
            weigh_values(1)
            logits(0)
            with pe.Fori(2, T - 1) as t:
                turn_probs(t)
                scores(t + 1)
                pe.wait_ge(logit_ready, t - 1)
                turn_xf(t - 1)
                weigh_values(t)
                logits(t - 1)
            turn_probs(T - 1)
            pe.wait_ge(logit_ready, T - 2)
            turn_xf(T - 2)
            weigh_values(T - 1)
            logits(T - 2)
            pe.wait_ge(logit_ready, T - 1)
            turn_xf(T - 1)
            logits(T - 1)

            pe.wait_ge(member_ready, 1)
            flat = T * E
            pe.matmul(psum[:, 0, 0:flat], before, member.rearrange("p t e -> p (t e)"), start=True, stop=False)
            pe.matmul(psum[:, 0, 0:flat], ones, earlier.rearrange("p t e -> p (t e)"), start=False, stop=True)
            pe.matmul(psum[:, 0, flat:flat + E], ones, earlier[:, T - 1, :], start=True, stop=False)
            pe.matmul(psum[:, 0, flat:flat + E], ones[0:TAIL, :], member[0:TAIL, T - 1, :],
                      start=False, stop=True).then_inc(rank_done, 1)
            pe.wait_ge(expert_hot_ready, 1)
            pe.wait_ge(b1_loaded, 16)
            for c in range(FC):
                m = pe.matmul(psum[:, 2, c * SLOT_TILES:(c + 1) * SLOT_TILES], b1_rows[:, c * P:(c + 1) * P],
                              expert_hot[:], start=True, stop=True)
            m.then_inc(b1_done, 1)
            pe.wait_ge(hot_ready, 1)
            for a in range(T * K):
                rows = TAIL if a // K == T - 1 else P
                m = pe.matmul(psum[:, 1, 0:SLOT_TILES], row_hot[0:rows, a, :], blk_hot[0:rows, a, :],
                              start=(a == 0), stop=(a == T * K - 1))
            m.then_inc(slots_done, 1)

            def turn_x(i):
                pe.wait_ge(x_gathered, 16 * i + 16)
                for c in range(DC):
                    m = pe.transpose(psum[:, 5, c * P:(c + 1) * P], x_slot[:, c * P:(c + 1) * P], ident[:])
                m.then_inc(xT_done, 1)

            def expert_of(i):
                return pe.value_load(tile_expert_i[0:1, bass.ds(i, 1)], min_val=0, max_val=E - 1)

            def layer1(i, e):
                pe.wait_ge(xT_ready, i + 1)
                for b in range(HB):
                    for c in range(DC):
                        m = pe.matmul(psum[:, b, :], xT_slot[:, c, :],
                                      w1_sb[:, bass.ds(e, 1), c, b * BANK:(b + 1) * BANK],
                                      start=(c == 0), stop=(c == DC - 1))
                m.then_inc(h_done, 1)

            def turn_h(i):
                pe.wait_ge(h_copied, i + 1)
                for c in range(FC):
                    m = pe.transpose(psum[:, 2 + c // CHUNKS_PER_BANK,
                                          c % CHUNKS_PER_BANK * P:(c % CHUNKS_PER_BANK + 1) * P],
                                     h_sb[:, c * P:(c + 1) * P], ident[:])
                m.then_inc(hT_done, 1)

            def layer2(i, e):
                pe.wait_ge(hT_ready, i + 1)
                for c in range(FC):
                    m = pe.matmul(psum[:, 4, 0:D], hT_sb[:, c, :], w2_sb[:, bass.ds(e, 1), c, :],
                                  start=(c == 0), stop=(c == FC - 1))
                m.then_inc(z_done, 1)

            pe.wait_ge(slots_ready, 1)
            pe.wait_ge(expert_loaded, 32 * E)
            turn_x(0)
            layer1(0, expert_of(0))
            turn_x(1)
            pe.wait_ge(b1_ready, 1)
            turn_h(0)
            e_now, e_before = expert_of(1), expert_of(0)
            layer1(1, e_now)
            turn_x(2)
            layer2(0, e_before)
            turn_h(1)
            with pe.Fori(2, SLOT_TILES - 1) as i:
                e_now, e_before = expert_of(i), expert_of(i - 1)
                layer1(i, e_now)
                turn_x(i + 1)
                pe.wait_ge(z_read, i - 1)
                layer2(i - 1, e_before)
                turn_h(i)
            last = SLOT_TILES - 1
            layer1(last, expert_of(last))
            pe.wait_ge(z_read, last - 1)
            layer2(last - 1, expert_of(last - 1))
            turn_h(last)
            pe.wait_ge(z_read, last)
            layer2(last, expert_of(last))

        @block.vector
        def _(dve):
            def hold():
                dve.memset(held[:, 0:1], 0.0)

            dve.memset(x_res[64:P, T - 1, :], 0.0).then_inc(pad_zeroed, 1)
            dve.memset(minus_half[:], -0.5).then_inc(dve_setup, 1)
            dve.wait_ge(iotas, 1)
            dve.tensor_scalar(ident[:], col[:], part[:, 0:1], None, ALU.is_equal).then_inc(consts, 1)

            def row(a):
                return a.rearrange("p a d -> p (a d)")

            def find_moments(t):
                dve.bn_stats(stats[:], row(x_res[:, bass.ds(t, 1), :])).then_inc(moment_step, 1)
                dve.wait_ge(moment_step, 2 * t + 1)
                hold()
                dve.bn_aggr(moments2[:], stats[:]).then_inc(moment_step, 1)
                dve.wait_ge(moment_step, 2 * t + 2)
                dve.tensor_scalar(mean[:, bass.ds(t, 1)], moments2[:, 0:1], 1.0, None, ALU.mult)
                dve.tensor_scalar(var_eps[:, bass.ds(t, 1)], moments2[:, 1:2], LN_EPS, None, ALU.add)\
                    .then_inc(moments_ready, 1)

            def normalise(t):
                dve.wait_ge(rstd_ready, t + 1)
                dve.tensor_scalar(xn, row(x_res[:, bass.ds(t, 1), :]), mean[:, bass.ds(t, 1)],
                                  rstd[:, bass.ds(t, 1)], ALU.subtract, ALU.mult).then_inc(xn_ready, 1)

            def take_qkv(t):
                dve.wait_ge(qkv_done, t + 1)
                banks = psum[:, bass.ds(1 + t % 2, 1), :]
                for o in range(DC):
                    dve.tensor_scalar(kT[:, o, bass.ds(t * P, P)], row(banks[:, :, (DC + o) * P:(DC + o + 1) * P]),
                                      bias_qk[:, 1, o:o + 1], None, ALU.add)
                for o in range(DC):
                    dve.tensor_scalar(qT[:, o, bass.ds(t * P, P)], row(banks[:, :, o * P:(o + 1) * P]),
                                      bias_qk[:, 0, o:o + 1], QK_SCALE, ALU.add, ALU.mult)
                dve.tensor_scalar(v_sb[:, bass.ds(t, 1), :], psum[:, bass.ds(3 + t % 2, 1), 0:D], 1.0, None,
                                  ALU.mult).then_inc(qkv_ready, 1)

            dve.wait_ge(x_loaded, 48)
            for t in range(3):
                find_moments(t)
                if t == 0:
                    normalise(0)
            dve.wait_ge(xnT_done, 1)
            normalise(1)
            dve.wait_ge(small_loaded, 48)
            with dve.Fori(0, T - 3) as t:
                find_moments(t + 3)
                dve.wait_ge(xnT_done, t + 2)
                normalise(t + 2)
                take_qkv(t)
            dve.wait_ge(xnT_done, T - 1)
            normalise(T - 1)
            for t in range(T - 3, T):
                take_qkv(t)

            dve.wait_ge(qkv_done, T)
            dve.memset(ones, 1.0)
            dve.tensor_scalar(before, col[:], part[:, 0:1], None, ALU.is_gt)

            def take_scores(t, u):
                dve.wait_ge(adj_loaded[u], 8 * (t - u) + 16)
                dve.wait_ge(s_done, t + 1)
                hold()
                dve.tensor_tensor_reduce(adj_sb[:, u, :], psum[:, 0:len(KEY_BANKS), :]
                                         .rearrange("p b n -> p (b n)")[:, 0:N], adj_sb[:, u, :], 2.0, LEAST,
                                         ALU.add, ALU.max, row_max[:]).then_inc(softmax_step, 1)
                dve.wait_ge(softmax_step, t + 1)
                dve.tensor_scalar(neg_max[:], row_max[:], -1.0, None, ALU.mult).then_inc(max_ready, 1)

            def take_probs(t):
                dve.wait_ge(pT_done, t + 1)
                dve.tensor_copy(probT[:, CHUNKS_PER_BANK:2 * CHUNKS_PER_BANK, :].rearrange("p j n -> p (j n)"),
                                psum[:, 4, :]).then_inc(pT_by_dve, 1)
                dve.reciprocal(row_inv[:], row_sum[:]).then_inc(inv_ready, 1)

            def take_logit(t):
                dve.wait_ge(logits_done, t + 1)
                dve.tensor_scalar(logit[:, bass.ds(t, 1), :], psum[:, 7:8, D:D + E], 1.0, None, ALU.mult)\
                    .then_inc(logit_ready, 1)

            def finish(t):
                xt = row(x_res[:, bass.ds(t, 1), :])
                dve.wait_ge(pv_done, t + 1)
                dve.wait_ge(inv_ready, t + 1)
                dve.scalar_tensor_tensor(xt, psum[:, 6, 0:D], row_inv[:, 0:1], xt, ALU.mult, ALU.add)\
                    .then_inc(finish_step, 1)
                dve.wait_ge(finish_step, 3 * t + 1)
                hold()
                dve.bn_stats(stats2[:], xt).then_inc(finish_step, 1)
                dve.wait_ge(finish_step, 3 * t + 2)
                hold()
                dve.bn_aggr(moments2[:], stats2[:]).then_inc(finish_step, 1)
                dve.wait_ge(finish_step, 3 * t + 3)
                dve.tensor_scalar(var2[:], moments2[:, 1:2], LN_EPS, None, ALU.add).then_inc(moments2_ready, 1)
                dve.wait_ge(rstd2_ready, t + 1)
                dve.tensor_scalar(xf_now[:], xt, moments2[:, 0:1], rstd2[:, 0:1], ALU.subtract, ALU.mult)\
                    .then_inc(xf_ready, 1)

            def attend(t, u):
                take_probs(t)
                take_scores(t + 1, 1 - u)
                dve.wait_ge(xfT_done, t)
                dve.wait_ge(xf_stored, 16 * t)
                finish(t)
                take_logit(t - 1)

            dve.wait_ge(bv_added, T)
            take_scores(0, 0)
            take_probs(0)
            take_scores(1, 1)
            finish(0)
            with dve.Fori(1, T - 3, 2) as i:
                attend(i, 1)
                attend(i + 1, 0)
            attend(T - 2, 1)
            take_probs(T - 1)
            dve.wait_ge(xfT_done, T - 1)
            dve.wait_ge(xf_stored, 16 * (T - 1))
            finish(T - 1)
            take_logit(T - 2)
            take_logit(T - 1)

            steps = [0]

            def link(ins):
                steps[0] += 1
                ins.then_inc(route_step, 1)
                dve.wait_ge(route_step, steps[0])

            def per_expert(a):
                return a.unsqueeze(2).broadcast_to((P, T, E))

            experts = expert_no[:].unsqueeze(1).broadcast_to((P, T, E))
            dve.wait_ge(logit_ready, T)
            dve.wait_ge(spare_ready, 1)
            left = logit[:]
            for k in range(K):
                link(dve.tensor_reduce(best[:, :, k], left, AX.X, ALU.max))
                link(dve.tensor_tensor(is_best, left, per_expert(best[:, :, k]), ALU.not_equal))
                link(dve.scalar_tensor_tensor(is_best, is_best, float(E), experts, ALU.mult, ALU.add))
                link(dve.tensor_reduce(where_best, is_best, AX.X, ALU.min))
                link(dve.tensor_tensor(hot[:, :, k, :], experts, per_expert(where_best), ALU.is_equal))
                if k == 0:
                    link(dve.scalar_tensor_tensor(rest, hot[:, :, 0, :], LEAST, left, ALU.mult, ALU.add))
                    left = rest
            link(dve.tensor_tensor(member, hot[:, :, 0, :], hot[:, :, 1, :], ALU.add))
            link(dve.memset(earlier[:, 0, :], 0.0))
            for t in range(1, T):
                m = dve.tensor_tensor(earlier[:, t, :], earlier[:, t - 1, :], member[:, t - 1, :], ALU.add)
                if t < T - 1:
                    link(m)
            m.then_inc(member_ready, 1)
            dve.tensor_tensor(gate_tmp[:, 0], best[:, :, 1], best[:, :, 0], ALU.subtract).then_inc(gap_ready, 1)
            dve.wait_ge(rank_done, 1)
            counts = psum[:, 0, T * E:T * E + E].unsqueeze(2).broadcast_to((P, E, T))
            link(dve.tensor_tensor(tile_cmp, counts, tile_edges[:].unsqueeze(1).broadcast_to((P, E, T)), ALU.is_gt))
            link(dve.tensor_reduce(tiles_of[:], tile_cmp, AX.X, ALU.add))
            link(dve.tensor_tensor(start_cmp, lower[:], tiles_of[:].unsqueeze(1).broadcast_to((P, E, E)), ALU.mult))
            link(dve.tensor_reduce(block_start[:], start_cmp, AX.X, ALU.add))
            link(dve.scalar_tensor_tensor(slot_base, block_start[:].unsqueeze(1).broadcast_to((P, T, E)), float(P),
                                          psum[:, 0, 0:T * E].rearrange("p (t e) -> p t e", e=E),
                                          ALU.mult, ALU.add))
            for k in range(K):
                m = dve.tensor_tensor(slot_pick.rearrange("p (t k) e -> p t k e", k=K)[:, :, k, :],
                                      hot[:, :, k, :], slot_base, ALU.mult)
            link(m)
            link(dve.tensor_reduce(slot_f, slot_pick, AX.X, ALU.add))
            link(dve.tensor_copy(slot_i, slot_f))
            dve.tensor_scalar(slot_row_i, slot_i, P - 1, None, ALU.bitwise_and)
            link(dve.tensor_scalar(slot_blk_i, slot_i, P.bit_length() - 1, None, ALU.logical_shift_right))
            dve.tensor_copy(slot_row, slot_row_i)
            link(dve.tensor_copy(slot_blk, slot_blk_i))
            link(dve.tensor_tensor(blk_hot, spare_col[:].unsqueeze(1).broadcast_to((P, T * K, SLOT_TILES)),
                                   slot_blk.unsqueeze(2).broadcast_to((P, T * K, SLOT_TILES)), ALU.is_equal))
            dve.tensor_tensor(blk_hot, blk_hot, pair_no[:].rearrange("p t k -> p (t k)").unsqueeze(2)
                              .broadcast_to((P, T * K, SLOT_TILES)), ALU.mult)
            dve.tensor_tensor(row_hot, col[:].unsqueeze(1).broadcast_to((P, T * K, P)),
                              slot_row.unsqueeze(2).broadcast_to((P, T * K, P)), ALU.is_equal).then_inc(hot_ready, 1)
            link(dve.tensor_tensor(expert_cmp, spare_col[:].unsqueeze(2).broadcast_to((P, SLOT_TILES, E - 1)),
                                   block_start[:, 1:E].unsqueeze(1).broadcast_to((P, SLOT_TILES, E - 1)),
                                   ALU.is_ge))
            link(dve.tensor_reduce(tile_expert[:], expert_cmp, AX.X, ALU.add))
            dve.tensor_scalar(expert_hot[:], tile_expert[0:E, :], part[0:E, 0:1], None, ALU.is_equal)\
                .then_inc(expert_hot_ready, 1)
            dve.tensor_copy(tile_expert_i[:], tile_expert[:])
            dve.wait_ge(slots_done, 1)
            found = psum[:, 1, 0:SLOT_TILES]
            link(dve.scalar_tensor_tensor(slot_tmp, found, 0.0, spare[:], ALU.is_equal, ALU.mult))
            dve.scalar_tensor_tensor(slot_pair[:], found, -1.0, slot_tmp, ALU.add, ALU.max)
            link(dve.tensor_scalar(slot_tok_i, found, -1.0, 0.0, ALU.add, ALU.max))
            dve.tensor_scalar(slot_token[:], slot_tok_i, K.bit_length() - 1, None, ALU.logical_shift_right)\
                .then_inc(slots_ready, 1)
            dve.wait_ge(b1_done, 1)
            dve.tensor_copy(b1_tiles.rearrange("p i c -> p c i"),
                            psum[:, 2, 0:FC * SLOT_TILES].rearrange("p (c i) -> p c i", c=FC)).then_inc(b1_ready, 1)
            dve.wait_ge(gap_exp, 1)
            link(dve.tensor_scalar(gate_tmp[:, 2], gate_tmp[:, 1], 1.0, None, ALU.add))
            link(dve.reciprocal(gates[:, :, 0], gate_tmp[:, 2]))
            dve.tensor_tensor(gates[:, :, 1], gate_tmp[:, 1], gates[:, :, 0], ALU.mult).then_inc(gate_ready, 1)

            def take_h(i):
                dve.wait_ge(h_done, i + 1)
                for b in range(HB):
                    m = dve.tensor_copy(h_sb[:, b * BANK:(b + 1) * BANK], psum[:, b, :])
                m.then_inc(h_copied, 1)

            def take_xT(i):
                dve.wait_ge(xT_done, i + 1)
                dve.tensor_copy(xT_slot.rearrange("p c n -> p (c n)"), psum[:, 5, 0:D]).then_inc(xT_ready, 1)

            def finish_tile(i):
                norm = norm_sb[:, bass.ds(i % NORM_RING, 1)]
                dve.wait_ge(xb_ready, i + 1)
                dve.wait_ge(z_done, i + 1)
                dve.tensor_tensor(y_sum, psum[:, 4, 0:D], row(xb_slot[:, bass.ds(i % XB_RING, 1), :]), ALU.add)\
                    .then_inc(z_read, 1)
                dve.wait_ge(z_read, i + 1)
                dve.bn_stats(stats2[:], y_sum).then_inc(y_step, 1)
                dve.wait_ge(y_step, 3 * i + 1)
                hold()
                dve.bn_aggr(moments2[:], stats2[:]).then_inc(y_step, 1)
                dve.wait_ge(y_step, 3 * i + 2)
                dve.tensor_scalar(var2[:], moments2[:, 1:2], EXPERT_EPS, None, ALU.add).then_inc(y_moments, 1)
                dve.scalar_tensor_tensor(y_mid, y_sum, moments2[:, 0:1], norm[:, :, 1, :].rearrange("p a d -> p (a d)"),
                                         ALU.subtract, ALU.mult).then_inc(y_step, 1)
                dve.wait_ge(y_step, 3 * i + 3)
                dve.wait_ge(y_rstd, i + 1)
                dve.scalar_tensor_tensor(y_out, y_mid, rstd2[:, 0:1], norm[:, :, 2, :].rearrange("p a d -> p (a d)"),
                                         ALU.mult, ALU.add).then_inc(y_ready, 1)

            take_xT(0)
            take_h(0)
            take_xT(1)
            dve.wait_ge(hT_done, 1)
            take_h(1)
            take_xT(2)
            finish_tile(0)
            with dve.Fori(2, SLOT_TILES - 1) as i:
                dve.wait_ge(hT_done, i)
                take_h(i)
                take_xT(i + 1)
                dve.wait_ge(pair_stored, 16 * i - 16)
                finish_tile(i - 1)
            last = SLOT_TILES - 1
            dve.wait_ge(hT_done, last)
            take_h(last)
            dve.wait_ge(pair_stored, 16 * last - 16)
            finish_tile(last - 1)
            dve.wait_ge(pair_stored, 16 * last)
            finish_tile(last)

            dve.wait_ge(pair_loaded, 16 * 4)
            with dve.Fori(0, T) as t:
                xt = row(x_res[:, bass.ds(t, 1), :])
                dve.scalar_tensor_tensor(xt, row(pair_sb[:, bass.ds(t, 1), 0, :]),
                                         row(gates[:, bass.ds(t, 1), 0:1]), xt, ALU.mult, ALU.add)\
                    .then_inc(out_step, 1)
                dve.wait_ge(out_step, t + 1)
                dve.scalar_tensor_tensor(xt, row(pair_sb[:, bass.ds(t, 1), 1, :]),
                                         row(gates[:, bass.ds(t, 1), 1:2]), xt, ALU.mult, ALU.add)\
                    .then_inc(out_ready, 1)

        @block.scalar
        def _(act):
            def take_xnT(t, u):
                act.wait_ge(xnT_done, t + 1)
                act.activation(xnT[:, u].rearrange("p c n -> p (c n)"), psum[:, 0, 0:D], ACT.Copy)\
                    .then_inc(xnT_ready, 1)

            take_xnT(0, 0)
            take_xnT(1, 1)
            with act.Fori(2, T - 2, 2) as i:
                for u in range(2):
                    act.wait_ge(qkv_done, i + u - 1)
                    take_xnT(i + u, u)
            act.wait_ge(qkv_done, T - 2)
            take_xnT(T - 1, 0)

            def exponentials(t, u):
                act.wait_ge(max_ready, t + 1)
                act.activation(prob[:], adj_sb[:, u, :], ACT.Exp, bias=neg_max[:, 0:1], accum_out=row_sum[:, 0:1])\
                    .then_inc(p_ready, 1)

            def take_probs(t):
                act.wait_ge(pT_done, t + 1)
                rest_chunks = T - 2 * CHUNKS_PER_BANK
                rows = N - (T - 1) * P
                act.activation(probT[:, 0:CHUNKS_PER_BANK, :].rearrange("p j n -> p (j n)"), psum[:, 3, :], ACT.Copy)
                act.activation(probT[:, 2 * CHUNKS_PER_BANK:T - 1, :].rearrange("p j n -> p (j n)"),
                               psum[:, 5, 0:(rest_chunks - 1) * P], ACT.Copy)
                act.activation(probT[0:rows, T - 1, :], psum[0:rows, 5, (rest_chunks - 1) * P:rest_chunks * P],
                               ACT.Copy).then_inc(pT_by_act, 1)

            def take_xfT(t):
                act.wait_ge(xfT_done, t + 1)
                act.activation(xfT[:].rearrange("p c n -> p (c n)"), psum[:, 7, 0:D], ACT.Copy)\
                    .then_inc(xfT_ready, 1)

            def attend(t, u):
                take_probs(t)
                act.wait_ge(inv_ready, t + 1)
                exponentials(t + 1, 1 - u)
                take_xfT(t - 1)

            exponentials(0, 0)
            take_probs(0)
            act.wait_ge(inv_ready, 1)
            exponentials(1, 1)
            with act.Fori(1, T - 3, 2) as i:
                attend(i, 1)
                attend(i + 1, 0)
            attend(T - 2, 1)
            take_probs(T - 1)
            take_xfT(T - 2)
            take_xfT(T - 1)

            act.wait_ge(gap_ready, 1)
            act.activation(gate_tmp[:, 1], gate_tmp[:, 0], ACT.Exp).then_inc(gap_exp, 1)

            act.wait_ge(slots_ready, 1)
            act.wait_ge(b1_ready, 1)
            act.wait_ge(pv_done, T)

            def expert_of(i):
                return act.value_load(tile_expert_i[0:1, bass.ds(i, 1)], min_val=0, max_val=E - 1)

            def load_norm(i, e):
                act.dma_start(norm_sb[:, bass.ds(i % NORM_RING, 1)],
                              norm_rows[bass.ds(e, 1)].broadcast_to((P, 3, D))
                              .rearrange("p (r a) d -> p r a d", r=1)).then_inc(norm_loaded, 16)

            def take_hT(i):
                act.wait_ge(hT_done, i + 1)
                bias = b1_tiles[:, bass.ds(i, 1), :].rearrange("p i c -> p (i c)")
                for c in range(FC):
                    m = act.activation(hT_sb[:, c, :], psum[:, 2 + c // CHUNKS_PER_BANK,
                                                            c % CHUNKS_PER_BANK * P:(c % CHUNKS_PER_BANK + 1) * P],
                                       ACT.Relu, bias=bias[:, c:c + 1])
                m.then_inc(hT_ready, 1)

            load_norm(0, expert_of(0))
            act.wait_ge(norm_loaded, 16)
            load_norm(1, expert_of(1))
            for i in range(NORM_RING - 2):
                take_hT(i)
                act.wait_ge(norm_loaded, 16 * i + 32)
                load_norm(i + 2, expert_of(i + 2))
            with act.Fori(NORM_RING - 2, SLOT_TILES - 2) as i:
                take_hT(i)
                e = expert_of(i + 2)
                act.wait_ge(norm_loaded, 16 * i + 32)
                act.wait_ge(y_ready, i + 3 - NORM_RING)
                load_norm(i + 2, e)
            take_hT(SLOT_TILES - 2)
            take_hT(SLOT_TILES - 1)

        @block.gpsimd
        def _(pool):
            def hold():
                pool.tensor_tensor(held[:, 1:2], minus_half[:, 0:1], minus_half[:, 0:1], ALU.mult)

            pool.iota(col[:], [[1, P]], base=0, channel_multiplier=0, allow_small_or_imprecise_dtypes=True)
            pool.iota(part[:], [[1, 1]], base=0, channel_multiplier=1, allow_small_or_imprecise_dtypes=True)\
                .then_inc(iotas, 1)
            pool.wait_ge(dve_setup, 1)

            with pool.Fori(0, T) as t:
                pool.wait_ge(moments_ready, t + 1)
                pool.tensor_tensor(rstd[:, bass.ds(t, 1)], var_eps[:, bass.ds(t, 1)], minus_half[:, bass.ds(t, 1)],
                                   ALU.pow).then_inc(rstd_ready, 1)
            pool.iota(pair_no[:], [[K * P, T], [1, K]], base=1, channel_multiplier=K,
                      allow_small_or_imprecise_dtypes=True)
            pool.iota(spare[:], [[P, SLOT_TILES]], base=PAIRS, channel_multiplier=1,
                      allow_small_or_imprecise_dtypes=True)
            pool.iota(spare_col[:], [[1, SLOT_TILES]], base=0, channel_multiplier=0,
                      allow_small_or_imprecise_dtypes=True)
            pool.iota(tile_edges[:], [[P, T]], base=0, channel_multiplier=0, allow_small_or_imprecise_dtypes=True)
            pool.iota(expert_no[:], [[1, E]], base=0, channel_multiplier=0, allow_small_or_imprecise_dtypes=True)
            pool.iota(order[:], [[1, E], [-1, E]], base=0, channel_multiplier=0,
                      allow_small_or_imprecise_dtypes=True).then_inc(pool_step, 1)
            pool.wait_ge(pool_step, 1)
            pool.tensor_scalar(lower[:], order[:], 0.0, None, ALU.is_gt).then_inc(spare_ready, 1)

            pool.wait_ge(small_loaded, 48)
            with pool.Fori(0, T) as t:
                pool.wait_ge(xn_ready, t + 1)
                pool.tensor_tensor(x_res[:, bass.ds(t, 1), :], x_res[:, bass.ds(t, 1), :],
                                   bv_rows[:].unsqueeze(1), ALU.add).then_inc(bv_added, 1)

            def copy_q(t):
                pool.tensor_copy(q_now[:], qT[:, :, bass.ds(t * P, P)]).then_inc(q_copied, 1)

            def rsqrt(t, ready, done):
                pool.wait_ge(ready, t + 1)
                pool.tensor_tensor(rstd2[:], var2[:], minus_half[:, 0:1], ALU.pow).then_inc(done, 1)

            pool.wait_ge(qkv_ready, T)
            copy_q(0)
            pool.wait_ge(s_done, 1)
            copy_q(1)
            with pool.Fori(0, T - 2) as t:
                pool.wait_ge(s_done, t + 2)
                copy_q(t + 2)
                rsqrt(t, moments2_ready, rstd2_ready)
            rsqrt(T - 2, moments2_ready, rstd2_ready)
            rsqrt(T - 1, moments2_ready, rstd2_ready)

            def gather(i):
                pool.tensor_copy(token_now[:], slot_token[:, bass.ds(i, 1)]).then_inc(token_ready, 1)
                pool.wait_ge(token_ready, i + 1)
                hold()
                pool.indirect_dma_start(x_slot, None, xf_dram, bass.IndirectOffsetOnAxis(ap=token_now[:, 0:1], axis=0))\
                    .then_inc(x_gathered, 16)

            def add_bias(i):
                pool.wait_ge(norm_loaded, 16 * i + 16)
                pool.wait_ge(xT_done, i + 1)
                pool.tensor_tensor(xb_slot[:, bass.ds(i % XB_RING, 1), :], x_slot.unsqueeze(1),
                                   norm_sb[:, bass.ds(i % NORM_RING, 1), 0, :], ALU.add).then_inc(xb_ready, 1)
                pool.wait_ge(xb_ready, i + 1)

            def scatter(i):
                rsqrt(i, y_moments, y_rstd)
                pool.tensor_copy(pair_now[:], slot_pair[:, bass.ds(i, 1)]).then_inc(index_ready, 1)
                pool.wait_ge(index_ready, i + 1)
                pool.wait_ge(y_ready, i + 1)
                hold()
                pool.indirect_dma_start(pair_dram, bass.IndirectOffsetOnAxis(ap=pair_now[:, 0:1], axis=0), y_out, None)\
                    .then_inc(pair_stored, 16)

            pool.wait_ge(slots_ready, 1)
            pool.wait_ge(xf_stored, 16 * T)
            gather(0)
            add_bias(0)
            gather(1)
            add_bias(1)
            gather(2)
            add_bias(2)
            gather(3)
            scatter(0)
            with pool.Fori(3, SLOT_TILES - 1) as i:
                add_bias(i)
                gather(i + 1)
                pool.wait_ge(pair_stored, 16 * i - 32)
                scatter(i - 2)
            last = SLOT_TILES - 1
            add_bias(last)
            for i in range(last - 2, SLOT_TILES):
                pool.wait_ge(pair_stored, 16 * i)
                scatter(i)


_INS = ["x", "adj", "wqT", "wkT", "wvT", "bias_cols", "bv", "router_w", "w1", "b1", "w2", "norm_rows"]


def kernel(x, adj, L0_gnn_Wq, L0_gnn_bq, L0_gnn_Wk, L0_gnn_bk, L0_gnn_Wv, L0_gnn_bv, L0_ffn_router_w, L0_ffn_w1,
           L0_ffn_b1, L0_ffn_w2, L0_ffn_b2, L0_ffn_gamma, L0_ffn_beta):
    import concourse.bacc as bacc
    from concourse.bass_utils import run_bass_kernel_spmd

    rows = [np.asarray(a) for a in (L0_ffn_b2, L0_ffn_gamma, L0_ffn_beta)]
    given = dict(x=x, adj=adj, wqT=np.asarray(L0_gnn_Wq).T, wkT=np.asarray(L0_gnn_Wk).T, wvT=np.asarray(L0_gnn_Wv).T,
                 bias_cols=np.stack([L0_gnn_bq, L0_gnn_bk]).reshape(2, -1, P).transpose(2, 0, 1), bv=L0_gnn_bv, router_w=L0_ffn_router_w, w1=L0_ffn_w1, b1=L0_ffn_b1,
                 w2=L0_ffn_w2, norm_rows=np.stack(rows, axis=1))
    nc = bacc.Bacc("TRN2", target_bir_lowering=False, num_devices=1)
    arrays, args = {}, []
    for name in _INS:
        a = np.ascontiguousarray(given[name])
        arrays[name] = a
        args.append(nc.dram_tensor(name, a.shape, mybir.dt.from_np(a.dtype), kind="ExternalInput").ap())
    out = nc.dram_tensor("out", arrays["x"].shape, F32, kind="ExternalOutput").ap()
    block_kernel(nc, *args, out)
    r = run_bass_kernel_spmd(nc, [arrays], core_ids=[0])
    return r.results[0]["out"]
```

```python
from contextlib import ExitStack

import numpy as np

import concourse.bass as bass
from concourse import mybir

F32 = mybir.dt.float32
I32 = mybir.dt.int32
F32R = mybir.dt.float32r
BF16 = mybir.dt.bfloat16
ALU = mybir.AluOpType
ACT = mybir.ActivationFunctionType
AX = mybir.AxisListType

P = 128
BANK = 512
LN_EPS = 1e-5
EXPERT_EPS = 1e-6
LEAST = -3.0e38


def block_kernel(nc, x, adj, wqT, wkT, wvT, bias_cols, bv, router_w, w1, b1, w2, norm_rows, out):
    N, D = x.shape
    E, _, F = w1.shape
    K = 2
    T = (N + P - 1) // P
    TAIL = N - (T - 1) * P
    NP = T * P
    DC = D // P
    FC = F // P
    HB = F // BANK
    SLOT_TILES = (K * N + E * (P - 1)) // P
    TK = T * K
    PARTS = 3
    TELL = SLOT_TILES + SLOT_TILES % 2
    HALVES = [(0, T // 2), (T // 2, T)]
    KEY_BANKS = [(b, min(BANK, N - b)) for b in range(0, N, BANK)]
    CHUNKS_PER_BANK = BANK // P
    QK_SCALE = float(D) ** -0.5 / 2

    xf_dram = nc.dram_tensor("xf_rows", (N, D), F32, kind="Internal").ap()
    sum_dram = nc.dram_tensor("sum_rows", (N + P, D), F32, kind="Internal").ap()

    with ExitStack() as ctx:
        arena_at = -(-nc.sbuf_base // 32) * 32
        ctx.enter_context(nc.sbuf_tensor("arena", [P, (nc.sbuf_usable_end - arena_at) // 64 * 64 // 4], F32))
        end = [arena_at]
        start_of = {}

        def place(name, shape, dt=F32, over=None):
            size = -(-int(np.prod(shape[1:])) * (2 if dt == BF16 else 4) // 32) * 32
            if over is None:
                at = end[0]
                end[0] += size
                assert end[0] <= nc.sbuf_usable_end, (name, end[0] - nc.sbuf_usable_end)
            else:
                base, skip = over if isinstance(over, tuple) else (over, 0)
                at = start_of[base] + skip
            start_of[name] = at
            start_of[name + " end"] = at + size
            return nc.alloc_sbuf_tensor_at(name, list(shape), dt, offset=at)

        def chain(base, things):
            made, last = [], base
            for name, shape, dt in things:
                made.append(place(name, shape, dt, over=last))
                last = name + " end"
            return made

        def sem(name):
            return ctx.enter_context(nc.semaphore(name))

        psum = ctx.enter_context(nc.psum_tensor("psum", [P, 8, BANK], F32))

        w1_sb = place("w1_sb", [P, E, DC, F])
        w2_sb = place("w2_sb", [P, E, FC, D])
        x_res = place("x_res", [P, T, D])
        qT = place("qT", [P, DC, NP])
        k_hi = place("k_hi", [P, DC, NP], F32R)
        v_hi = place("v_hi", [P, T, D], F32R)
        adj_sb = place("adj_sb", [P, 2, N])
        prob = place("prob", [P, N])
        pT_hi = place("pT_hi", [P, T, P], F32R)
        wqkv = place("wqkv", [P, 3, DC, D])
        xf_now = place("xf_now", [P, D])
        xfT = place("xfT", [P, DC, P])
        bias_qk = place("bias_qk", [P, 2, DC])
        bv_rows = place("bv_rows", [P, D])
        router = place("router", [P, DC, E])
        LATE = E // 2
        k_lo, v_lo, pT_lo, q_hi, q_lo = chain(("w2_sb", LATE * FC * D * 4), [
            ("k_lo", [P, DC, NP], F32R), ("v_lo", [P, T, D], F32R), ("pT_lo", [P, T, P], F32R),
            ("q_hi", [P, DC, P], F32R), ("q_lo", [P, DC, P], F32R)])
        assert start_of["q_lo end"] <= start_of["w2_sb end"]
        xn, xnT = chain("prob", [("xn", [P, D], F32), ("xnT", [P, 2, DC, P], F32)])
        assert start_of["xnT end"] <= start_of["prob end"]
        b1_rows, before, ones, member = chain("wqkv", [
            ("b1_rows", [E, F], F32),
            ("before", [P, P], BF16),
            ("ones", [P, P], BF16), ("member", [P, T, E], BF16)])
        assert start_of["member end"] <= start_of["wqkv end"]
        b1_tiles = place("b1_tiles", [P, SLOT_TILES, FC], over="bv_rows")
        assert start_of["b1_tiles end"] <= start_of["bv_rows end"]
        stats = place("stats", [P, 6])
        moments = place("moments", [P, 2])
        mean = place("mean", [P, T])
        var_eps = place("var_eps", [P, T])
        rstd = place("rstd", [P, T])
        minus_half = place("minus_half", [P, T])
        stats2 = place("stats2", [P, 6])
        moments2 = place("moments2", [P, 2])
        var2 = place("var2", [P, 1])
        rstd2 = place("rstd2", [P, 1])
        row_max = place("row_max", [P, 1])
        neg_max = place("neg_max", [P, 1])
        row_sum = place("row_sum", [P, 1])
        row_inv = place("row_inv", [P, 1])
        logit = place("logit", [P, T, E])
        held_dve = place("held_dve", [P, 1])
        held_pool = place("held_pool", [P, 1])
        ident = place("ident", [P, P])
        col = place("col", [P, P])
        part = place("part", [P, 1])
        tile_no = place("tile_no", [P, TELL])
        token_no = place("token_no", [P, T])
        spare = place("spare", [P, 1])
        tile_edges = place("tile_edges", [P, T])
        expert_no = place("expert_no", [P, E])
        order = place("order", [P, E, E])
        lower = place("lower", [P, E, E])
        tile_expert_i = place("tile_expert_i", [P, SLOT_TILES], I32)
        expert_hot = place("expert_hot", [E, SLOT_TILES])
        slot_row = place("slot_row", [P, SLOT_TILES], I32)
        slot_token = place("slot_token", [P, SLOT_TILES], I32)
        slot_gate = place("slot_gate", [P, SLOT_TILES])
        row_now = place("row_now", [P, 1], I32)
        token_now = place("token_now", [P, 1], I32)

        (row_hot, blk_hot, hot, best, rest, is_best, where_best, slot_base, slot_pick, slot_f, slot_i, slot_low_i,
         slot_blk_i, slot_low, slot_blk, tile_cmp, tiles_of, start_cmp, block_start, expert_cmp, tile_expert,
         blk_is, slot_tmp, gate_tmp, gates, gate_hi, gate_lo) = chain("qT", [
            ("row_hot", [P, TK, P], F32R),
            ("blk_hot", [P, TK, PARTS, TELL], F32R),
            ("hot", [P, T, K, E], F32), ("best", [P, T, K], F32), ("rest", [P, T, E], F32),
            ("is_best", [P, T, E], F32), ("where_best", [P, T], F32), ("slot_base", [P, T, E], F32),
            ("slot_pick", [P, TK, E], F32), ("slot_f", [P, TK], F32), ("slot_i", [P, TK], I32),
            ("slot_low_i", [P, TK], I32), ("slot_blk_i", [P, TK], I32), ("slot_low", [P, TK], F32),
            ("slot_blk", [P, TK], F32), ("tile_cmp", [P, E, T], F32), ("tiles_of", [P, E], F32),
            ("start_cmp", [P, E, E], F32), ("block_start", [P, E], F32),
            ("expert_cmp", [P, SLOT_TILES, E - 1], F32), ("tile_expert", [P, SLOT_TILES], F32),
            ("blk_is", [P, TK, TELL], F32), ("slot_tmp", [P, SLOT_TILES], F32),
            ("gate_tmp", [P, 3, T], F32), ("gates", [P, T, K], F32), ("gate_hi", [P, TK], F32R),
            ("gate_lo", [P, TK], F32)])
        assert start_of["gate_lo end"] <= start_of["v_hi end"]
        NORM_RING = XB_RING = 4
        norm_sb, hT_sb, xb_slot, y_out = chain("x_res", [
            ("norm_sb", [P, NORM_RING, 3, D], F32),
            ("hT_sb", [P, 2, FC, P], F32), ("xb_slot", [P, XB_RING, D], F32), ("y_out", [P, D], F32)])
        assert start_of["y_out end"] <= start_of["adj_sb"]
        w1_now, x_slot, xT_slot, y_sum, y_mid = chain("adj_sb", [
            ("w1_now", [P, 2, DC, F], F32), ("x_slot", [P, D], F32), ("xT_slot", [P, DC, P], F32),
            ("y_sum", [P, D], F32), ("y_mid", [P, D], F32)])
        assert start_of["y_mid end"] <= start_of["pT_hi end"]

        x0_loaded = sem("x0_loaded")
        x_loaded = sem("x_loaded")
        w_loaded = sem("w_loaded")
        small_loaded = sem("small_loaded")
        adj_loaded = [sem("adj_loaded_even"), sem("adj_loaded_odd")]
        b1_loaded = sem("b1_loaded")
        expert_loaded = sem("expert_loaded")
        late_loaded = sem("late_loaded")
        xf_stored = sem("xf_stored")
        x1_stored = sem("x1_stored")
        norm_loaded = sem("norm_loaded")
        x_gathered = sem("x_gathered")
        sum_added = sem("sum_added")
        out_stored = sem("out_stored")
        pad_zeroed = sem("pad_zeroed")
        iotas = sem("iotas")
        consts = sem("consts")
        routing_consts = sem("routing_consts")
        moments_ready = sem("moments_ready")
        rstd_ready = sem("rstd_ready")
        xn_ready = sem("xn_ready")
        bv_added = sem("bv_added")
        xnT_done = sem("xnT_done")
        xnT_ready = sem("xnT_ready")
        kv_done = sem("kv_done")
        kv_hi_ready = sem("kv_hi_ready")
        q_done = sem("q_done")
        qkv_ready = sem("qkv_ready")
        q_hi_ready = sem("q_hi_ready")
        q_ready = sem("q_ready")
        s_done = sem("s_done")
        max_ready = sem("max_ready")
        p_ready = sem("p_ready")
        pT_done = sem("pT_done")
        pT_hi_ready = sem("pT_hi_ready")
        pT_lo_ready = sem("pT_lo_ready")
        inv_ready = sem("inv_ready")
        pv_done = sem("pv_done")
        x1_ready = sem("x1_ready")
        moments2_ready = sem("moments2_ready")
        rstd2_ready = sem("rstd2_ready")
        xf_ready = sem("xf_ready")
        xfT_done = sem("xfT_done")
        xfT_ready = sem("xfT_ready")
        logits_done = sem("logits_done")
        logit_ready = sem("logit_ready")
        gap_ready = sem("gap_ready")
        gap_exp = sem("gap_exp")
        member_ready = sem("member_ready")
        rank_done = sem("rank_done")
        hot_ready = sem("hot_ready")
        expert_hot_ready = sem("expert_hot_ready")
        experts_ready = sem("experts_ready")
        b1_done = sem("b1_done")
        b1_ready = sem("b1_ready")
        slots_done = sem("slots_done")
        slots_ready = sem("slots_ready")
        token_ready = sem("token_ready")
        xb_ready = sem("xb_ready")
        xT_done = sem("xT_done")
        xT_ready = sem("xT_ready")
        w1_ready = sem("w1_ready")
        h_done = sem("h_done")
        hT_ready = sem("hT_ready")
        z_done = sem("z_done")
        z_read = sem("z_read")
        y_moments = sem("y_moments")
        y_rstd = sem("y_rstd")
        y_ready = sem("y_ready")
        index_ready = sem("index_ready")
        dve_setup = sem("dve_setup")
        moment_step = sem("moment_step")
        softmax_step = sem("softmax_step")
        finish_step = sem("finish_step")
        route_step = sem("route_step")
        y_step = sem("y_step")
        pool_step = sem("pool_step")

        block = ctx.enter_context(nc.Block())

        PT_PARTS = []
        for b in range(0, T, CHUNKS_PER_BANK):
            whole = min(b + CHUNKS_PER_BANK, T - 1)
            PT_PARTS.append([(b // CHUNKS_PER_BANK, 0, b, whole, P)])
            if b + CHUNKS_PER_BANK >= T:
                PT_PARTS[-1].append((b // CHUNKS_PER_BANK, (T - 1 - b) * P, T - 1, T, TAIL))
        PT_BANKS = len(PT_PARTS)

        def turned(bank, at, a, b, rows):
            return psum[0:rows, 3 + bank, at:at + (b - a) * P]

        def chunks(tensor, a, b, rows):
            return tensor[0:rows, a:b, :].rearrange("p j n -> p (j n)")

        def row(a):
            return a.rearrange("p a d -> p (a d)")

        @block.sync
        def _(sp):
            sp.dma_start(x_res[:, 0, :], x[0:P, :]).then_inc(x0_loaded, 16)
            sp.dma_start(wqkv[:, 1], wkT.rearrange("(c p) o -> p c o", p=P)).then_inc(w_loaded, 16)
            sp.dma_start(wqkv[:, 2], wvT.rearrange("(c p) o -> p c o", p=P)).then_inc(w_loaded, 16)
            sp.dma_start(wqkv[:, 0], wqT.rearrange("(c p) o -> p c o", p=P)).then_inc(w_loaded, 16)
            sp.dma_start(x_res[:, 1:T - 1, :], x[P:(T - 1) * P, :].rearrange("(t p) d -> p t d", p=P))\
                .then_inc(x_loaded, 16)
            sp.wait_ge(pad_zeroed, 1)
            sp.dma_start(x_res[0:TAIL, T - 1, :], x[(T - 1) * P:N, :]).then_inc(x_loaded, 16)
            sp.dma_start(bias_qk[:], bias_cols).then_inc(small_loaded, 16)
            sp.dma_start(bv_rows[:, :], bv.rearrange("(a d) -> a d", a=1).broadcast_to((P, D)))\
                .then_inc(small_loaded, 16)
            sp.dma_start(router[:, :, :], router_w.rearrange("(c p) e -> p c e", p=P)).then_inc(small_loaded, 16)
            for u in range(2):
                sp.dma_start(adj_sb[:, u, :], adj[u * P:(u + 1) * P, :]).then_inc(adj_loaded[u], 16)
            with sp.Fori(0, E) as e:
                sp.dma_start(w1_sb[:, bass.ds(e, 1)], w1[bass.ds(e, 1)].rearrange("a (c p) f -> p a c f", p=P))\
                    .then_inc(expert_loaded, 16)
            sp.wait_ge(q_done, T)
            sp.dma_start(b1_rows[:], b1).then_inc(b1_loaded, 16)

            def load_w2(e, loaded):
                sp.dma_start(w2_sb[:, bass.ds(e, 1)], w2[bass.ds(e, 1)].rearrange("a (c p) d -> p a c d", p=P))\
                    .then_inc(loaded, 16)

            def store_tile(t, rows):
                sp.wait_ge(x1_ready, t + 1)
                sp.dma_start(sum_dram[bass.ds(t * P, rows), :], row(x_res[0:rows, bass.ds(t, 1), :]))\
                    .then_inc(x1_stored, 16)
                sp.wait_ge(xf_ready, t + 1)
                sp.dma_start(xf_dram[bass.ds(t * P, rows), :], xf_now[0:rows, :]).then_inc(xf_stored, 16)

            def load_adj(t, u, rows):
                sp.wait_ge(p_ready, t - 1)
                sp.dma_start(adj_sb[0:rows, u, :], adj[bass.ds(t * P, rows), :]).then_inc(adj_loaded[u], 16)

            assert 2 * LATE == E == T - 3
            with sp.Fori(0, LATE) as j:
                for u in range(2):
                    load_adj(j * 2 + u + 2, u, P)
                    if u == 0:
                        load_w2(j, expert_loaded)
                    store_tile(j * 2 + u, P)
            load_adj(T - 1, (T - 1) % 2, TAIL)
            sp.dma_start(sum_dram[N:N + P, :], x_res[:, 0, :]).then_inc(x1_stored, 16)
            for t in range(E, T - 1):
                store_tile(t, P)
            sp.wait_ge(pv_done, T)
            with sp.Fori(LATE, E) as e:
                load_w2(e, late_loaded)
            store_tile(T - 1, TAIL)

            sp.wait_ge(sum_added, 16 * SLOT_TILES)
            sp.dma_start(out, sum_dram[0:N, :]).then_inc(out_stored, 16)
            sp.wait_ge(out_stored, 16)

        @block.tensor
        def _(pe):
            pe.wait_ge(consts, 1)

            def turn_xn(t):
                pe.wait_ge(xn_ready, t + 1)
                for c in range(DC):
                    m = pe.transpose(psum[:, 0, c * P:(c + 1) * P], xn[:, c * P:(c + 1) * P], ident[:])
                m.then_inc(xnT_done, 1)

            def project(t, u):
                pe.wait_ge(xnT_ready, t + 1)
                for w, bank, done in ((1, 1 + u, kv_done), (0, 3 + u, q_done)):
                    if w == 1:
                        for c in range(DC):
                            pe.matmul(psum[:, bank, D:2 * D], xnT[:, u, c, :], wqkv[:, 2, c, :],
                                      start=(c == 0), stop=(c == DC - 1))
                    for o in range(DC):
                        for c in range(DC):
                            m = pe.matmul(psum[:, bank, o * P:(o + 1) * P], wqkv[:, w, c, o * P:(o + 1) * P],
                                          xnT[:, u, c, :], start=(c == 0), stop=(c == DC - 1))
                    m.then_inc(done, 1)

            turn_xn(0)
            pe.wait_ge(w_loaded, 48)
            pe.wait_ge(xnT_ready, 1)
            turn_xn(1)
            project(0, 0)
            pe.wait_ge(xnT_ready, 2)
            turn_xn(2)
            project(1, 1)
            with pe.Fori(2, T - 2, 2) as i:
                for u in range(2):
                    t = i + u
                    pe.wait_ge(xnT_ready, t + 1)
                    turn_xn(t + 1)
                    pe.wait_ge(qkv_ready, t - 1)
                    project(t, u)
            pe.wait_ge(qkv_ready, T - 2)
            project(T - 1, 0)

            def scores(t):
                pe.wait_ge(q_ready, t + 1)
                for b, (k0, kn) in enumerate(KEY_BANKS):
                    for c in range(DC):
                        for j, (q, k) in enumerate(((q_hi, k_hi), (q_hi, k_lo), (q_lo, k_hi))):
                            m = pe.matmul(psum[:, b, 0:kn], q[:, c, :], k[:, c, k0:k0 + kn],
                                          start=(c == 0 and j == 0), stop=(c == DC - 1 and j == 2))
                m.then_inc(s_done, 1)

            def turn_probs(t):
                pe.wait_ge(p_ready, t + 1)
                for j in range(T):
                    rows = min(P, N - j * P)
                    a = j % CHUNKS_PER_BANK * P
                    m = pe.transpose(psum[0:rows, 3 + j // CHUNKS_PER_BANK, a:a + P],
                                     prob[:, j * P:j * P + rows], ident[:])
                m.then_inc(pT_done, 1)

            def weigh(p, v, first, last):
                for j in range(T):
                    rows = min(P, N - j * P)
                    m = pe.matmul(psum[:, 6, 0:D], p[0:rows, j, :], v[0:rows, j, :],
                                  start=(first and j == 0), stop=(last and j == T - 1))
                return m

            def weigh_high(t):
                pe.wait_ge(pT_hi_ready, PT_BANKS * t + PT_BANKS)
                weigh(pT_hi, v_hi, True, False)
                weigh(pT_hi, v_lo, False, False)

            def weigh_low(t):
                pe.wait_ge(pT_lo_ready, t + 1)
                weigh(pT_lo, v_hi, False, True).then_inc(pv_done, 1)

            def turn_xf(t):
                pe.wait_ge(xf_ready, t + 1)
                for c in range(DC):
                    m = pe.transpose(psum[:, 7, c * P:(c + 1) * P], xf_now[:, c * P:(c + 1) * P], ident[:])
                m.then_inc(xfT_done, 1)

            def logits(t):
                pe.wait_ge(xfT_ready, t + 1)
                for c in range(DC):
                    m = pe.matmul(psum[:, 7, D:D + E], xfT[:, c, :], router[:, c, :],
                                  start=(c == 0), stop=(c == DC - 1))
                m.then_inc(logits_done, 1)

            pe.wait_ge(qkv_ready, T)
            pe.wait_ge(small_loaded, 48)
            scores(0)
            turn_probs(0)
            scores(1)
            weigh_high(0)
            weigh_low(0)
            turn_probs(1)
            scores(2)
            turn_xf(0)
            weigh_high(1)
            logits(0)
            weigh_low(1)
            with pe.Fori(2, T - 1) as t:
                turn_probs(t)
                scores(t + 1)
                pe.wait_ge(logit_ready, t - 1)
                turn_xf(t - 1)
                weigh_high(t)
                logits(t - 1)
                weigh_low(t)
            turn_probs(T - 1)
            pe.wait_ge(logit_ready, T - 2)
            turn_xf(T - 2)
            weigh_high(T - 1)
            logits(T - 2)
            weigh_low(T - 1)
            pe.wait_ge(logit_ready, T - 1)
            turn_xf(T - 1)
            logits(T - 1)

            pe.wait_ge(member_ready, 1)
            flat = T * E
            members = member[:].rearrange("p t e -> p (t e)")
            pe.matmul(psum[:, 0, 0:flat], before[:], members, start=True, stop=False)
            for d in range(1, T):
                pe.matmul(psum[:, 0, d * E:flat], ones[:], members[:, 0:flat - d * E], start=False, stop=(d == T - 1))
            for t in range(T):
                rows = TAIL if t == T - 1 else P
                m = pe.matmul(psum[:, 0, flat:flat + E], ones[0:rows, :], member[0:rows, t, :],
                              start=(t == 0), stop=(t == T - 1))
            m.then_inc(rank_done, 1)
            for h, (t0, t1) in enumerate(HALVES):
                pe.wait_ge(hot_ready, h + 1)
                for a in range(t0 * K, t1 * K):
                    rows = TAIL if a // K == T - 1 else P
                    m = pe.matmul(psum[:, 1, 0:PARTS * TELL],
                                  row_hot[0:rows, a, :], blk_hot[0:rows, a].rearrange("p c s -> p (c s)"),
                                  start=(a == 0), stop=(a == TK - 1))
            m.then_inc(slots_done, 1)
            pe.wait_ge(expert_hot_ready, 1)
            pe.wait_ge(b1_loaded, 16)
            for c in range(FC):
                m = pe.matmul(psum[:, 2, c * SLOT_TILES:(c + 1) * SLOT_TILES], b1_rows[:, c * P:(c + 1) * P],
                              expert_hot[:], start=True, stop=True)
            m.then_inc(b1_done, 1)

            def turn_x(i):
                pe.wait_ge(x_gathered, 16 * i + 16)
                for c in range(DC):
                    m = pe.transpose(psum[:, 5, c * P:(c + 1) * P], x_slot[:, c * P:(c + 1) * P], ident[:])
                m.then_inc(xT_done, 1)

            def expert_of(i):
                return pe.value_load(tile_expert_i[0:1, bass.ds(i, 1)], min_val=0, max_val=E - 1)

            def layer1(i, u):
                pe.wait_ge(xT_ready, i + 1)
                pe.wait_ge(w1_ready, i + 1)
                for b in range(HB):
                    for f in range(CHUNKS_PER_BANK):
                        at = (b * CHUNKS_PER_BANK + f) * P
                        for c in range(DC):
                            m = pe.matmul(psum[:, 2 * u + b, f * P:(f + 1) * P], w1_now[:, u, c, at:at + P],
                                          xT_slot[:, c, :], start=(c == 0), stop=(c == DC - 1))
                    m.then_inc(h_done, 1)

            def layer2(i, u):
                e = expert_of(i)
                pe.wait_ge(hT_ready, i + 1)
                for c in range(FC):
                    m = pe.matmul(psum[:, 4, 0:D], hT_sb[:, u, c, :], w2_sb[:, bass.ds(e, 1), c, :],
                                  start=(c == 0), stop=(c == FC - 1))
                m.then_inc(z_done, 1)

            pe.wait_ge(slots_ready, 2)
            turn_x(0)
            layer1(0, 0)
            turn_x(1)
            pe.wait_ge(b1_ready, 1)
            layer1(1, 1)
            turn_x(2)
            pe.wait_ge(expert_loaded, 16 * (E + LATE))
            pe.wait_ge(late_loaded, 16 * (E - LATE))
            layer2(0, 0)
            with pe.Fori(2, SLOT_TILES - 2, 2) as i:
                for u in range(2):
                    layer1(i + u, u)
                    turn_x(i + u + 1)
                    pe.wait_ge(z_read, i + u - 1)
                    layer2(i + u - 1, 1 - u)
            last = SLOT_TILES - 1
            layer1(last, 0)
            pe.wait_ge(z_read, last - 1)
            layer2(last - 1, 1)
            pe.wait_ge(z_read, last)
            layer2(last, 0)

        @block.vector
        def _(dve):
            def hold():
                dve.memset(held_dve[:], 0.0)

            dve.memset(x_res[64:P, T - 1, :], 0.0).then_inc(pad_zeroed, 1)
            dve.memset(minus_half[:], -0.5).then_inc(dve_setup, 1)
            dve.wait_ge(iotas, 1)
            dve.tensor_scalar(ident[:], col[:], part[:, 0:1], None, ALU.is_equal).then_inc(consts, 1)

            def find_moments(t):
                dve.bn_stats(stats[:], row(x_res[:, bass.ds(t, 1), :])).then_inc(moment_step, 1)
                dve.wait_ge(moment_step, 2 * t + 1)
                hold()
                dve.bn_aggr(moments[:], stats[:]).then_inc(moment_step, 1)
                dve.wait_ge(moment_step, 2 * t + 2)
                dve.tensor_scalar(mean[:, bass.ds(t, 1)], moments[:, 0:1], 1.0, None, ALU.mult)
                dve.tensor_scalar(var_eps[:, bass.ds(t, 1)], moments[:, 1:2], LN_EPS, None, ALU.add)\
                    .then_inc(moments_ready, 1)

            def normalise(t):
                dve.wait_ge(rstd_ready, t + 1)
                dve.tensor_scalar(xn[:], row(x_res[:, bass.ds(t, 1), :]), mean[:, bass.ds(t, 1)],
                                  rstd[:, bass.ds(t, 1)], ALU.subtract, ALU.mult).then_inc(xn_ready, 1)

            def take_qkv(t):
                kv = psum[:, bass.ds(1 + t % 2, 1), :]
                q = psum[:, bass.ds(3 + t % 2, 1), :]
                dve.wait_ge(kv_hi_ready, t + 1)
                for o in range(DC):
                    at = bass.ds(t * P, P)
                    dve.scalar_tensor_tensor(k_lo[:, o, at], row(kv[:, :, o * P:(o + 1) * P]), bias_qk[:, 1, o:o + 1],
                                             k_hi[:, o, at].bitcast(F32), ALU.add, ALU.subtract)
                dve.scalar_tensor_tensor(v_lo[:, bass.ds(t, 1), :], kv[:, :, D:2 * D], 1.0,
                                         v_hi[:, bass.ds(t, 1), :].bitcast(F32), ALU.mult, ALU.subtract)
                dve.wait_ge(q_done, t + 1)
                for o in range(DC):
                    m = dve.tensor_scalar(qT[:, o, bass.ds(t * P, P)], row(q[:, :, o * P:(o + 1) * P]),
                                          bias_qk[:, 0, o:o + 1], QK_SCALE, ALU.add, ALU.mult)
                m.then_inc(qkv_ready, 1)

            dve.wait_ge(x0_loaded, 16)
            find_moments(0)
            normalise(0)
            dve.wait_ge(x_loaded, 32)
            find_moments(1)
            find_moments(2)
            dve.wait_ge(xnT_done, 1)
            normalise(1)
            dve.wait_ge(small_loaded, 48)
            with dve.Fori(0, T - 3) as t:
                find_moments(t + 3)
                dve.wait_ge(xnT_done, t + 2)
                normalise(t + 2)
                take_qkv(t)
            dve.wait_ge(xnT_done, T - 1)
            normalise(T - 1)
            for t in range(T - 3, T):
                take_qkv(t)

            dve.wait_ge(q_done, T)
            dve.memset(ones[:], 1.0)
            dve.tensor_scalar(before[:], col[:], part[:, 0:1], None, ALU.is_gt)

            def take_q(t):
                dve.wait_ge(q_hi_ready, t + 1)
                dve.scalar_tensor_tensor(q_lo[:], qT[:, :, bass.ds(t * P, P)], 1.0, q_hi[:].bitcast(F32),
                                         ALU.mult, ALU.subtract).then_inc(q_ready, 1)

            def take_scores(t, u):
                dve.wait_ge(adj_loaded[u], 8 * (t - u) + 16)
                dve.wait_ge(s_done, t + 1)
                hold()
                dve.tensor_tensor_reduce(adj_sb[:, u, :], psum[:, 0:len(KEY_BANKS), :]
                                         .rearrange("p b n -> p (b n)")[:, 0:N], adj_sb[:, u, :], 2.0, LEAST,
                                         ALU.add, ALU.max, row_max[:]).then_inc(softmax_step, 1)
                dve.wait_ge(softmax_step, t + 1)
                dve.tensor_scalar(neg_max[:], row_max[:], -1.0, None, ALU.mult).then_inc(max_ready, 1)

            def take_probs(t):
                for b, parts in enumerate(PT_PARTS):
                    dve.wait_ge(pT_hi_ready, PT_BANKS * t + b + 1)
                    for bank, at, c0, c1, rows in parts:
                        m = dve.tensor_tensor(chunks(pT_lo, c0, c1, rows), turned(bank, at, c0, c1, rows),
                                              chunks(pT_hi, c0, c1, rows).bitcast(F32), ALU.subtract)
                m.then_inc(pT_lo_ready, 1)
                dve.reciprocal(row_inv[:], row_sum[:]).then_inc(inv_ready, 1)

            def take_logit(t):
                dve.wait_ge(logits_done, t + 1)
                dve.tensor_scalar(logit[:, bass.ds(t, 1), :], psum[:, 7:8, D:D + E], 1.0, None, ALU.mult)\
                    .then_inc(logit_ready, 1)

            def add_attention(t):
                xt = row(x_res[:, bass.ds(t, 1), :])
                dve.wait_ge(pv_done, t + 1)
                dve.wait_ge(inv_ready, t + 1)
                dve.scalar_tensor_tensor(xt, psum[:, 6, 0:D], row_inv[:, 0:1], xt, ALU.mult, ALU.add)\
                    .then_inc(x1_ready, 1)
                dve.wait_ge(x1_ready, t + 1)
                hold()
                dve.bn_stats(stats2[:], xt).then_inc(finish_step, 1)
                dve.wait_ge(finish_step, 2 * t + 1)
                hold()
                dve.bn_aggr(moments2[:], stats2[:]).then_inc(finish_step, 1)
                dve.wait_ge(finish_step, 2 * t + 2)
                dve.tensor_scalar(var2[:], moments2[:, 1:2], LN_EPS, None, ALU.add).then_inc(moments2_ready, 1)

            def norm_x(t, first=False):
                if not first:
                    dve.wait_ge(xfT_done, t)
                    dve.wait_ge(xf_stored, 16 * t)
                dve.wait_ge(rstd2_ready, t + 1)
                dve.tensor_scalar(xf_now[:], row(x_res[:, bass.ds(t, 1), :]), moments2[:, 0:1], rstd2[:, 0:1],
                                  ALU.subtract, ALU.mult).then_inc(xf_ready, 1)

            def attend(t, u, first=False):
                add_attention(t - 1)
                take_probs(t)
                norm_x(t - 1, first)
                take_scores(t + 1, 1 - u)

            dve.wait_ge(bv_added, T)
            take_q(0)
            take_scores(0, 0)
            take_q(1)
            take_probs(0)
            take_scores(1, 1)
            take_q(2)
            attend(1, 1, first=True)
            take_q(3)
            take_logit(0)
            with dve.Fori(2, T - 4, 2) as i:
                for u in range(2):
                    attend(i + u, u)
                    take_q(i + u + 2)
                    take_logit(i + u - 1)
            attend(T - 3, 0)
            take_q(T - 1)
            take_logit(T - 4)
            attend(T - 2, 1)
            take_logit(T - 3)
            add_attention(T - 2)
            take_probs(T - 1)
            norm_x(T - 2)
            take_logit(T - 2)
            add_attention(T - 1)
            norm_x(T - 1)
            take_logit(T - 1)

            steps = [0]

            def link(ins):
                steps[0] += 1
                ins.then_inc(route_step, 1)
                dve.wait_ge(route_step, steps[0])

            def per_expert(a):
                return a.unsqueeze(2).broadcast_to((P, T, E))

            experts = expert_no[:].unsqueeze(1).broadcast_to((P, T, E))
            dve.wait_ge(logit_ready, T)
            dve.wait_ge(routing_consts, 1)
            left = logit[:]
            for k in range(K):
                link(dve.tensor_reduce(best[:, :, k], left, AX.X, ALU.max))
                link(dve.tensor_tensor(is_best[:], left, per_expert(best[:, :, k]), ALU.not_equal))
                link(dve.scalar_tensor_tensor(is_best[:], is_best[:], float(E), experts, ALU.mult, ALU.add))
                link(dve.tensor_reduce(where_best[:], is_best[:], AX.X, ALU.min))
                link(dve.tensor_tensor(hot[:, :, k, :], experts, per_expert(where_best[:]), ALU.is_equal))
                if k == 0:
                    link(dve.scalar_tensor_tensor(rest[:], hot[:, :, 0, :], LEAST, left, ALU.mult, ALU.add))
                    left = rest[:]
            dve.tensor_tensor(member[:], hot[:, :, 0, :], hot[:, :, 1, :], ALU.add).then_inc(member_ready, 1)
            dve.tensor_tensor(gate_tmp[:, 0], best[:, :, 1], best[:, :, 0], ALU.subtract).then_inc(gap_ready, 1)
            dve.wait_ge(gap_exp, 1)
            link(dve.tensor_scalar(gate_tmp[:, 2], gate_tmp[:, 1], 1.0, None, ALU.add))
            link(dve.reciprocal(gates[:, :, 0], gate_tmp[:, 2]))
            link(dve.tensor_tensor(gates[:, :, 1], gate_tmp[:, 1], gates[:, :, 0], ALU.mult))
            gate_flat = gates[:].rearrange("p t k -> p (t k)")
            link(dve.tensor_copy(gate_hi[:], gate_flat))
            dve.tensor_tensor(gate_lo[:], gate_flat, gate_hi[:].bitcast(F32), ALU.subtract)
            dve.wait_ge(rank_done, 1)
            counts = psum[:, 0, T * E:T * E + E].unsqueeze(2).broadcast_to((P, E, T))
            link(dve.tensor_tensor(tile_cmp[:], counts, tile_edges[:].unsqueeze(1).broadcast_to((P, E, T)), ALU.is_gt))
            link(dve.tensor_reduce(tiles_of[:], tile_cmp[:], AX.X, ALU.add))
            link(dve.tensor_tensor(start_cmp[:], lower[:], tiles_of[:].unsqueeze(1).broadcast_to((P, E, E)), ALU.mult))
            link(dve.tensor_reduce(block_start[:], start_cmp[:], AX.X, ALU.add))
            link(dve.scalar_tensor_tensor(slot_base[:], block_start[:].unsqueeze(1).broadcast_to((P, T, E)), float(P),
                                          psum[:, 0, 0:T * E].rearrange("p (t e) -> p t e", e=E),
                                          ALU.mult, ALU.add))
            for k in range(K):
                m = dve.tensor_tensor(slot_pick[:].rearrange("p (t k) e -> p t k e", k=K)[:, :, k, :],
                                      hot[:, :, k, :], slot_base[:], ALU.mult)
            link(m)
            link(dve.tensor_reduce(slot_f[:], slot_pick[:], AX.X, ALU.add))
            link(dve.tensor_copy(slot_i[:], slot_f[:]))
            dve.tensor_scalar(slot_low_i[:], slot_i[:], P - 1, None, ALU.bitwise_and)
            link(dve.tensor_scalar(slot_blk_i[:], slot_i[:], P.bit_length() - 1, None, ALU.logical_shift_right))
            dve.tensor_copy(slot_low[:], slot_low_i[:])
            link(dve.tensor_copy(slot_blk[:], slot_blk_i[:]))
            for t0, t1 in HALVES:
                a0, a1 = t0 * K, t1 * K
                shape = (P, a1 - a0, TELL)
                link(dve.tensor_tensor(blk_is[:, a0:a1], tile_no[:].unsqueeze(1).broadcast_to(shape),
                                       slot_blk[:, a0:a1].unsqueeze(2).broadcast_to(shape), ALU.is_equal))
                for k in range(K):
                    dve.tensor_tensor(blk_hot[:].rearrange("p (t k) c s -> p t k c s", k=K)[:, t0:t1, k, 0],
                                      blk_is[:].rearrange("p (t k) s -> p t k s", k=K)[:, t0:t1, k],
                                      token_no[:, t0:t1].unsqueeze(2).broadcast_to((P, t1 - t0, TELL)), ALU.mult)
                dve.tensor_tensor(blk_hot[:, a0:a1, 1], blk_is[:, a0:a1],
                                  gate_hi[:, a0:a1].bitcast(F32).unsqueeze(2).broadcast_to(shape), ALU.mult)
                dve.tensor_tensor(blk_hot[:, a0:a1, 2], blk_is[:, a0:a1],
                                  gate_lo[:, a0:a1].unsqueeze(2).broadcast_to(shape), ALU.mult)
                dve.tensor_tensor(row_hot[:, a0:a1], col[:].unsqueeze(1).broadcast_to((P, a1 - a0, P)),
                                  slot_low[:, a0:a1].unsqueeze(2).broadcast_to((P, a1 - a0, P)), ALU.is_equal)\
                    .then_inc(hot_ready, 1)
            link(dve.tensor_tensor(expert_cmp[:], tile_no[:, 0:SLOT_TILES].unsqueeze(2)
                                   .broadcast_to((P, SLOT_TILES, E - 1)),
                                   block_start[:, 1:E].unsqueeze(1).broadcast_to((P, SLOT_TILES, E - 1)),
                                   ALU.is_ge))
            link(dve.tensor_reduce(tile_expert[:], expert_cmp[:], AX.X, ALU.add))
            dve.tensor_scalar(expert_hot[:], tile_expert[0:E, :], part[0:E, 0:1], None, ALU.is_equal)\
                .then_inc(expert_hot_ready, 1)
            dve.tensor_copy(tile_expert_i[:], tile_expert[:]).then_inc(experts_ready, 1)
            dve.wait_ge(slots_done, 1)
            found = psum[:, 1, 0:SLOT_TILES]
            dve.tensor_scalar(slot_token[:], found, -1.0, 0.0, ALU.add, ALU.max).then_inc(slots_ready, 1)
            link(dve.tensor_scalar(slot_tmp[:], found, 0.0, spare[:, 0:1], ALU.is_equal, ALU.mult))
            dve.scalar_tensor_tensor(slot_row[:], found, -1.0, slot_tmp[:], ALU.add, ALU.max)
            dve.tensor_reduce(slot_gate[:], psum[:, 1, TELL:3 * TELL].rearrange("p (c s) -> p s c", c=2)
                              [:, 0:SLOT_TILES, :], AX.X, ALU.add).then_inc(slots_ready, 1)
            def norm_of(i):
                return norm_sb[:, bass.ds(i % NORM_RING, 1)]

            def find_y_moments(i):
                dve.wait_ge(xb_ready, i + 1)
                dve.wait_ge(z_done, i + 1)
                dve.tensor_tensor(y_sum[:], psum[:, 4, 0:D], row(xb_slot[:, bass.ds(i % XB_RING, 1), :]), ALU.add)\
                    .then_inc(z_read, 1)
                dve.wait_ge(z_read, i + 1)
                dve.bn_stats(stats2[:], y_sum[:]).then_inc(y_step, 1)
                dve.wait_ge(y_step, 4 * i + 1)
                hold()
                dve.bn_aggr(moments2[:], stats2[:]).then_inc(y_step, 1)
                dve.wait_ge(y_step, 4 * i + 2)
                dve.tensor_scalar(var2[:], moments2[:, 1:2], EXPERT_EPS, None, ALU.add).then_inc(y_moments, 1)
                dve.scalar_tensor_tensor(y_mid[:], y_sum[:], moments2[:, 0:1],
                                         norm_of(i)[:, :, 1, :].rearrange("p a d -> p (a d)"),
                                         ALU.subtract, ALU.mult).then_inc(y_step, 1)

            def finish_y(i):
                dve.wait_ge(y_step, 4 * i + 3)
                dve.wait_ge(y_rstd, i + 1)
                dve.scalar_tensor_tensor(y_mid[:], y_mid[:], rstd2[:, 0:1],
                                         norm_of(i)[:, :, 2, :].rearrange("p a d -> p (a d)"),
                                         ALU.mult, ALU.add).then_inc(y_step, 1)
                dve.wait_ge(y_step, 4 * i + 4)
                dve.tensor_scalar(y_out[:], y_mid[:], slot_gate[:, bass.ds(i, 1)], None, ALU.mult)\
                    .then_inc(y_ready, 1)

            dve.wait_ge(b1_done, 1)
            dve.tensor_copy(b1_tiles[:].rearrange("p i c -> p c i"),
                            psum[:, 2, 0:FC * SLOT_TILES].rearrange("p (c i) -> p c i", c=FC)).then_inc(b1_ready, 1)
            find_y_moments(0)
            finish_y(0)
            with dve.Fori(1, SLOT_TILES) as i:
                find_y_moments(i)
                dve.wait_ge(sum_added, 16 * i)
                finish_y(i)

        @block.scalar
        def _(act):
            def take_xnT(t, u):
                act.wait_ge(xnT_done, t + 1)
                act.activation(xnT[:, u].rearrange("p c n -> p (c n)"), psum[:, 0, 0:D], ACT.Copy)\
                    .then_inc(xnT_ready, 1)

            def take_kv(t, u):
                act.wait_ge(kv_done, t + 1)
                act.activation(v_hi[:, bass.ds(t, 1), :], psum[:, 1 + u:2 + u, D:2 * D], ACT.Copy)
                for o in range(DC):
                    m = act.activation(k_hi[:, o, bass.ds(t * P, P)], psum[:, 1 + u, o * P:(o + 1) * P],
                                       ACT.Identity, bias=bias_qk[:, 1, o:o + 1])
                m.then_inc(kv_hi_ready, 1)

            take_xnT(0, 0)
            take_xnT(1, 1)
            act.wait_ge(small_loaded, 48)
            with act.Fori(0, T - 4, 2) as i:
                for u in range(2):
                    take_kv(i + u, u)
                    act.wait_ge(q_done, i + u + 1)
                    take_xnT(i + u + 2, u)
            take_kv(T - 3, 0)
            act.wait_ge(q_done, T - 2)
            take_xnT(T - 1, 0)
            take_kv(T - 2, 1)
            take_kv(T - 1, 0)

            def take_q(t):
                act.activation(q_hi[:], qT[:, :, bass.ds(t * P, P)], ACT.Copy).then_inc(q_hi_ready, 1)

            def exponentials(t, u):
                act.wait_ge(max_ready, t + 1)
                act.activation(prob[:], adj_sb[:, u, :], ACT.Exp, bias=neg_max[:, 0:1], accum_out=row_sum[:, 0:1])\
                    .then_inc(p_ready, 1)

            def take_probs(t):
                act.wait_ge(pT_done, t + 1)
                for parts in PT_PARTS:
                    for bank, at, c0, c1, rows in parts:
                        m = act.activation(chunks(pT_hi, c0, c1, rows), turned(bank, at, c0, c1, rows), ACT.Copy)
                    m.then_inc(pT_hi_ready, 1)

            def take_xfT(t):
                act.wait_ge(xfT_done, t + 1)
                act.activation(xfT[:].rearrange("p c n -> p (c n)"), psum[:, 7, 0:D], ACT.Copy)\
                    .then_inc(xfT_ready, 1)

            def attend(t, u, next_q=True):
                take_probs(t)
                if next_q:
                    act.wait_ge(s_done, t + 2)
                    take_q(t + 2)
                take_xfT(t - 1)
                act.wait_ge(inv_ready, t + 1)
                exponentials(t + 1, 1 - u)

            act.wait_ge(qkv_ready, T)
            take_q(0)
            act.wait_ge(s_done, 1)
            take_q(1)
            exponentials(0, 0)
            take_probs(0)
            act.wait_ge(s_done, 2)
            take_q(2)
            act.wait_ge(inv_ready, 1)
            exponentials(1, 1)
            with act.Fori(1, T - 3, 2) as i:
                attend(i, 1)
                attend(i + 1, 0)
            attend(T - 2, 1, next_q=False)
            take_probs(T - 1)
            take_xfT(T - 2)
            take_xfT(T - 1)

            act.wait_ge(gap_ready, 1)
            act.activation(gate_tmp[:, 1], gate_tmp[:, 0], ACT.Exp).then_inc(gap_exp, 1)

            act.wait_ge(experts_ready, 1)
            act.wait_ge(pv_done, T)
            act.wait_ge(expert_loaded, 16 * (E + LATE))

            def expert_of(i):
                return act.value_load(tile_expert_i[0:1, bass.ds(i, 1)], min_val=0, max_val=E - 1)

            def load_norm(i, e):
                act.dma_start(norm_sb[:, bass.ds(i % NORM_RING, 1)],
                              norm_rows[bass.ds(e, 1)].broadcast_to((P, 3, D))
                              .rearrange("p (r a) d -> p r a d", r=1)).then_inc(norm_loaded, 16)

            def take_w1(i, u):
                e = expert_of(i)
                act.activation(w1_now[:, u], w1_sb[:, bass.ds(e, 1)].rearrange("p e c f -> p (e c) f"), ACT.Copy)\
                    .then_inc(w1_ready, 1)

            def take_xT(i):
                act.wait_ge(xT_done, i + 1)
                act.activation(xT_slot[:].rearrange("p c n -> p (c n)"), psum[:, 5, 0:D], ACT.Copy)\
                    .then_inc(xT_ready, 1)

            def take_h(i, u, b):
                act.wait_ge(h_done, i * HB + b + 1)
                bias = row(b1_tiles[:, bass.ds(i, 1), :])
                for f in range(CHUNKS_PER_BANK):
                    c = b * CHUNKS_PER_BANK + f
                    m = act.activation(hT_sb[:, u, c, :], psum[:, 2 * u + b, f * P:(f + 1) * P],
                                       ACT.Relu, bias=bias[:, c:c + 1])
                return m

            def step(i, u, load=True, first=False, last=False):
                if not last:
                    take_w1(i + 1, 1 - u)
                if not first:
                    act.wait_ge(z_done, i - 1)
                take_h(i, u, 0)
                if not last:
                    take_xT(i + 1)
                take_h(i, u, 1).then_inc(hT_ready, 1)
                if load:
                    e = expert_of(i + 2)
                    act.wait_ge(norm_loaded, 16 * i + 32)
                    if not first:
                        act.wait_ge(y_ready, i - 1)
                    load_norm(i + 2, e)

            assert HB == 2 and NORM_RING == 4 and SLOT_TILES % 2 == 1
            take_w1(0, 0)
            act.wait_ge(slots_ready, 2)
            act.wait_ge(x1_stored, 16 * (T + 1))
            load_norm(0, expert_of(0))
            take_xT(0)
            act.wait_ge(norm_loaded, 16)
            load_norm(1, expert_of(1))
            act.wait_ge(b1_ready, 1)
            step(0, 0, first=True)
            step(1, 1, first=True)
            with act.Fori(2, SLOT_TILES - 4, 2) as i:
                step(i, 0)
                step(i + 1, 1)
            step(SLOT_TILES - 3, 0)
            step(SLOT_TILES - 2, 1, load=False)
            step(SLOT_TILES - 1, 0, load=False, last=True)

        @block.gpsimd
        def _(pool):
            def hold():
                pool.tensor_tensor(held_pool[:], minus_half[:, 0:1], minus_half[:, 0:1], ALU.mult)

            def iota(tensor, pattern, base, per_partition):
                return pool.iota(tensor[:], pattern, base=base, channel_multiplier=per_partition,
                                 allow_small_or_imprecise_dtypes=True)

            iota(col, [[1, P]], 0, 0)
            iota(part, [[1, 1]], 0, 1).then_inc(iotas, 1)
            pool.wait_ge(dve_setup, 1)

            with pool.Fori(0, T) as t:
                pool.wait_ge(moments_ready, t + 1)
                pool.tensor_tensor(rstd[:, bass.ds(t, 1)], var_eps[:, bass.ds(t, 1)], minus_half[:, bass.ds(t, 1)],
                                   ALU.pow).then_inc(rstd_ready, 1)
            iota(token_no, [[P, T]], 1, 1)
            iota(spare, [[1, 1]], N, 1)
            iota(tile_no, [[1, TELL]], 0, 0)
            iota(tile_edges, [[P, T]], 0, 0)
            iota(expert_no, [[1, E]], 0, 0)
            iota(order, [[1, E], [-1, E]], 0, 0).then_inc(pool_step, 1)
            pool.wait_ge(pool_step, 1)
            pool.tensor_scalar(lower[:], order[:], 0.0, None, ALU.is_gt).then_inc(routing_consts, 1)

            pool.wait_ge(small_loaded, 48)
            with pool.Fori(0, T) as t:
                pool.wait_ge(xn_ready, t + 1)
                pool.tensor_tensor(x_res[:, bass.ds(t, 1), :], x_res[:, bass.ds(t, 1), :],
                                   bv_rows[:].unsqueeze(1), ALU.add).then_inc(bv_added, 1)

            def rsqrt(t, ready, done):
                pool.wait_ge(ready, t + 1)
                pool.tensor_tensor(rstd2[:], var2[:], minus_half[:, 0:1], ALU.pow).then_inc(done, 1)

            with pool.Fori(0, T) as t:
                rsqrt(t, moments2_ready, rstd2_ready)

            def gather(i):
                pool.tensor_copy(token_now[:], slot_token[:, bass.ds(i, 1)]).then_inc(token_ready, 1)
                pool.wait_ge(token_ready, i + 1)
                hold()
                pool.indirect_dma_start(x_slot[:], None, xf_dram,
                                        bass.IndirectOffsetOnAxis(ap=token_now[:, 0:1], axis=0))\
                    .then_inc(x_gathered, 16)

            def add_bias(i):
                pool.wait_ge(norm_loaded, 16 * i + 16)
                pool.wait_ge(xT_done, i + 1)
                pool.tensor_tensor(xb_slot[:, bass.ds(i % XB_RING, 1), :], x_slot[:].unsqueeze(1),
                                   norm_sb[:, bass.ds(i % NORM_RING, 1), 0, :], ALU.add).then_inc(xb_ready, 1)
                pool.wait_ge(xb_ready, i + 1)

            def add_rows(i):
                pool.tensor_copy(row_now[:], slot_row[:, bass.ds(i, 1)]).then_inc(index_ready, 1)
                pool.wait_ge(index_ready, i + 1)
                pool.wait_ge(y_ready, i + 1)
                hold()
                pool.indirect_dma_start(sum_dram, bass.IndirectOffsetOnAxis(ap=row_now[:, 0:1], axis=0), y_out[:], None,
                                        compute_op=ALU.add).then_inc(sum_added, 16)

            pool.wait_ge(slots_ready, 1)
            pool.wait_ge(xf_stored, 16 * T)
            gather(0)
            for i in range(3):
                add_bias(i)
                gather(i + 1)
            rsqrt(0, y_moments, y_rstd)
            add_bias(3)
            gather(4)
            pool.wait_ge(slots_ready, 2)
            pool.wait_ge(x1_stored, 16 * (T + 1))
            add_rows(0)
            with pool.Fori(3, SLOT_TILES - 2) as i:
                rsqrt(i - 2, y_moments, y_rstd)
                add_bias(i + 1)
                gather(i + 2)
                pool.wait_ge(sum_added, 16 * i - 32)
                add_rows(i - 2)
            last = SLOT_TILES - 1
            for i in range(last - 3, SLOT_TILES):
                rsqrt(i, y_moments, y_rstd)
                if i == last - 3:
                    add_bias(last)
                pool.wait_ge(sum_added, 16 * i)
                add_rows(i)


_INS = ["x", "adj", "wqT", "wkT", "wvT", "bias_cols", "bv", "router_w", "w1", "b1", "w2", "norm_rows"]


def kernel(x, adj, L0_gnn_Wq, L0_gnn_bq, L0_gnn_Wk, L0_gnn_bk, L0_gnn_Wv, L0_gnn_bv, L0_ffn_router_w, L0_ffn_w1,
           L0_ffn_b1, L0_ffn_w2, L0_ffn_b2, L0_ffn_gamma, L0_ffn_beta):
    import concourse.bacc as bacc
    from concourse.bass_utils import run_bass_kernel_spmd

    rows = [np.asarray(a) for a in (L0_ffn_b2, L0_ffn_gamma, L0_ffn_beta)]
    given = dict(x=x, adj=adj, wqT=np.asarray(L0_gnn_Wq).T, wkT=np.asarray(L0_gnn_Wk).T, wvT=np.asarray(L0_gnn_Wv).T,
                 bias_cols=np.stack([L0_gnn_bq, L0_gnn_bk]).reshape(2, -1, P).transpose(2, 0, 1), bv=L0_gnn_bv, router_w=L0_ffn_router_w, w1=L0_ffn_w1, b1=L0_ffn_b1,
                 w2=L0_ffn_w2, norm_rows=np.stack(rows, axis=1))
    nc = bacc.Bacc("TRN2", target_bir_lowering=False, num_devices=1)
    arrays, args = {}, []
    for name in _INS:
        a = np.ascontiguousarray(given[name])
        arrays[name] = a
        args.append(nc.dram_tensor(name, a.shape, mybir.dt.from_np(a.dtype), kind="ExternalInput").ap())
    out = nc.dram_tensor("out", arrays["x"].shape, F32, kind="ExternalOutput").ap()
    block_kernel(nc, *args, out)
    r = run_bass_kernel_spmd(nc, [arrays], core_ids=[0])
    return r.results[0]["out"]
```

```python
from contextlib import ExitStack

import numpy as np

import concourse.bass as bass
from concourse import mybir

F32 = mybir.dt.float32
I32 = mybir.dt.int32
F32R = mybir.dt.float32r
U32 = mybir.dt.uint32
BF16 = mybir.dt.bfloat16
ALU = mybir.AluOpType
ACT = mybir.ActivationFunctionType
AX = mybir.AxisListType

P = 128
BANK = 512
LN_EPS = 1e-5
EXPERT_EPS = 1e-6
LEAST = -3.0e38


def block_kernel(nc, x, adj, wqT, wkT, wvT, bias_cols, bv, router_w, w1, b1, w2, norm_rows, out):
    N, D = x.shape
    E, _, F = w1.shape
    K = 2
    T = (N + P - 1) // P
    TAIL = N - (T - 1) * P
    NP = T * P
    DC = D // P
    FC = F // P
    HB = F // BANK
    SLOT_TILES = (K * N + E * (P - 1)) // P
    TK = T * K
    PARTS = 3
    TELL = SLOT_TILES + SLOT_TILES % 2
    ROUTE_STEPS = [(t, min(t + 3, T)) for t in range(0, T, 3)]
    KEY_BANKS = [(b, min(BANK, N - b)) for b in range(0, N, BANK)]
    CHUNKS_PER_BANK = BANK // P
    QK_SCALE = float(D) ** -0.5 / 2

    xf_dram = nc.dram_tensor("xf_rows", (N, D), F32, kind="Internal").ap()
    sum_dram = nc.dram_tensor("sum_rows", (N + P, D), F32, kind="Internal").ap()

    with ExitStack() as ctx:
        arena_at = -(-nc.sbuf_base // 32) * 32
        ctx.enter_context(nc.sbuf_tensor("arena", [P, (nc.sbuf_usable_end - arena_at) // 64 * 64 // 4], F32))
        end = [arena_at]
        start_of = {}

        def place(name, shape, dt=F32, over=None):
            size = -(-int(np.prod(shape[1:])) * (2 if dt == BF16 else 4) // 32) * 32
            if over is None:
                at = end[0]
                end[0] += size
                assert end[0] <= nc.sbuf_usable_end, (name, end[0] - nc.sbuf_usable_end)
            else:
                base, skip = over if isinstance(over, tuple) else (over, 0)
                at = start_of[base] + skip
            start_of[name] = at
            start_of[name + " end"] = at + size
            return nc.alloc_sbuf_tensor_at(name, list(shape), dt, offset=at)

        def chain(base, things):
            made, last = [], base
            for name, shape, dt in things:
                made.append(place(name, shape, dt, over=last))
                last = name + " end"
            return made

        def sem(name):
            return ctx.enter_context(nc.semaphore(name))

        psum = ctx.enter_context(nc.psum_tensor("psum", [P, 8, BANK], F32))

        w2_sb = place("w2_sb", [P, E, FC, D])
        norm_sb = place("norm_sb", [P, E, 3, D])
        x_res = place("x_res", [P, T, D])
        qT = place("qT", [P, DC, NP])
        k_hi = place("k_hi", [P, DC, NP], F32R)
        k_lo = place("k_lo", [P, DC, NP], F32R)
        v_hi = place("v_hi", [P, T, D], F32R)
        v_lo = place("v_lo", [P, T, D], F32R)
        adj_sb = place("adj_sb", [P, 2, N])
        prob = place("prob", [P, N])
        pT_hi = place("pT_hi", [P, T, P], F32R)
        pT_lo = place("pT_lo", [P, T, P], F32R)
        q_hi = place("q_hi", [P, DC, P], F32R)
        q_lo = place("q_lo", [P, DC, P], F32R)
        wqkv = place("wqkv", [P, 3, DC, D])
        xf_now = place("xf_now", [P, D])
        xfT = place("xfT", [P, DC, P])
        bias_qk = place("bias_qk", [P, 2, DC])
        bv_rows = place("bv_rows", [P, D])
        router = place("router", [P, DC, E])
        xn, xnT = chain("prob", [("xn", [P, D], F32), ("xnT", [P, 2, DC, P], F32)])
        assert start_of["xnT end"] <= start_of["prob end"]
        b1_rows, before, ones, member = chain("wqkv", [
            ("b1_rows", [E, F], F32),
            ("before", [P, P], BF16),
            ("ones", [P, P], BF16), ("member", [P, T, E], BF16)])
        assert start_of["member end"] <= start_of["wqkv end"]
        b1_tiles = place("b1_tiles", [P, SLOT_TILES, FC], over="bv_rows")
        assert start_of["b1_tiles end"] <= start_of["bv_rows end"]
        stats = place("stats", [P, 6])
        moments = place("moments", [P, 2])
        mean_var = place("mean_var", [P, T, 2])
        zero_eps = place("zero_eps", [P, 2])
        rstd = place("rstd", [P, T])
        minus_half = place("minus_half", [P, T])
        stats2 = place("stats2", [P, 6])
        moments2 = place("moments2", [P, 2])
        var2 = place("var2", [P, 1])
        rstd2 = place("rstd2", [P, 1])
        q_bias = place("q_bias", [P, DC])
        row_max = place("row_max", [P, 1])
        neg_max = place("neg_max", [P, 1])
        row_sum = place("row_sum", [P, 1])
        row_inv = place("row_inv", [P, 1])
        top = place("top", [P, 8])
        top_at = place("top_at", [P, 8], U32)
        best = place("best", [P, T, K])
        best_at = place("best_at", [P, T, K])
        held_dve = place("held_dve", [P, 1])
        held_pool = place("held_pool", [P, 1])
        ident = place("ident", [P, P])
        col = place("col", [P, P])
        part = place("part", [P, 1])
        tile_no = place("tile_no", [P, TELL])
        told = place("told", [P, TK, PARTS])
        spare = place("spare", [P, 1])
        tile_edges = place("tile_edges", [P, T])
        expert_no = place("expert_no", [P, E])
        order = place("order", [P, E, E])
        lower = place("lower", [P, E, E])
        tile_expert_i = place("tile_expert_i", [P, SLOT_TILES], I32)
        expert_hot = place("expert_hot", [E, SLOT_TILES])
        slot_row = place("slot_row", [P, SLOT_TILES], I32)
        slot_token = place("slot_token", [P, SLOT_TILES], I32)
        slot_gate = place("slot_gate", [P, SLOT_TILES])
        row_now = [place(f"row_now_{u}", [P, 1], I32) for u in range(2)]
        token_now = [place(f"token_now_{u}", [P, 1], I32) for u in range(2)]

        (row_hot, blk_hot, hot, slot_base, slot_pick, slot_f, slot_i, slot_low_i,
         slot_blk_i, slot_low, slot_blk, tile_cmp, tiles_of, start_cmp, block_start, expert_cmp,
         blk_is, slot_tmp, gate_tmp, gates, gate_hi) = chain("qT", [
            ("row_hot", [P, TK, P], F32R),
            ("blk_hot", [P, TK, PARTS, TELL], F32R),
            ("hot", [P, T, K, E], F32), ("slot_base", [P, T, E], F32),
            ("slot_pick", [P, TK, E], F32), ("slot_f", [P, TK], F32), ("slot_i", [P, TK], I32),
            ("slot_low_i", [P, TK], I32), ("slot_blk_i", [P, TK], I32), ("slot_low", [P, TK], F32),
            ("slot_blk", [P, TK], F32), ("tile_cmp", [P, E, T], F32), ("tiles_of", [P, E], F32),
            ("start_cmp", [P, E, E], F32), ("block_start", [P, E], F32),
            ("expert_cmp", [P, SLOT_TILES, E], F32),
            ("blk_is", [P, TK, TELL], F32), ("slot_tmp", [P, SLOT_TILES], F32),
            ("gate_tmp", [P, 3, T], F32), ("gates", [P, T, K], F32), ("gate_hi", [P, TK], F32R)])
        assert start_of["gate_hi end"] <= start_of["v_hi"]
        XB_RING = 4
        x_slot, xT_slot, xb_slot, y_sum, y_mid, y_out = chain("x_res", [
            ("x_slot", [P, 2, D], F32), ("xT_slot", [P, DC, P], F32), ("xb_slot", [P, XB_RING, D], F32),
            ("y_sum", [P, D], F32), ("y_mid", [P, D], F32), ("y_out", [P, 2, D], F32)])
        assert start_of["y_out end"] <= start_of["qT"]
        hT_sb, h_hi_even, h_hi_odd, h_lo_even, h_lo_odd = chain("qT", [
            ("hT_sb", [P, F], F32), ("h_hi_even", [P, FC, P], F32R), ("h_hi_odd", [P, FC, P], F32R),
            ("h_lo_even", [P, FC, P], F32R), ("h_lo_odd", [P, FC, P], F32R)])
        assert start_of["h_lo_odd end"] <= start_of["v_hi"]
        w1_now, w2_hi_even, w2_hi_odd, w2_lo_even, w2_lo_odd = chain("v_hi", [
            ("w1_now", [P, 2, DC, F], F32), ("w2_hi_even", [P, FC, D], F32R), ("w2_hi_odd", [P, FC, D], F32R),
            ("w2_lo_even", [P, FC, D], F32R), ("w2_lo_odd", [P, FC, D], F32R)])
        assert start_of["w2_lo_odd end"] <= start_of["pT_lo end"]
        h_hi, h_lo = (h_hi_even, h_hi_odd), (h_lo_even, h_lo_odd)
        w2_hi, w2_lo = (w2_hi_even, w2_hi_odd), (w2_lo_even, w2_lo_odd)

        x0_loaded = sem("x0_loaded")
        x12_loaded = sem("x12_loaded")
        x_loaded = sem("x_loaded")
        w_loaded = sem("w_loaded")
        small_loaded = sem("small_loaded")
        adj_loaded = [sem("adj_loaded_even"), sem("adj_loaded_odd")]
        b1_loaded = sem("b1_loaded")
        w2_loaded = sem("w2_loaded")
        w1_loaded = [sem("w1_loaded_even"), sem("w1_loaded_odd")]
        xf_stored = sem("xf_stored")
        x1_stored = sem("x1_stored")
        norm_loaded = sem("norm_loaded")
        x_gathered = [sem("x_gathered_even"), sem("x_gathered_odd")]
        sum_added = sem("sum_added")
        out_stored = sem("out_stored")
        pad_zeroed = sem("pad_zeroed")
        iotas = sem("iotas")
        consts = sem("consts")
        routing_consts = sem("routing_consts")
        moments_ready = sem("moments_ready")
        rstd_ready = sem("rstd_ready")
        xn_ready = sem("xn_ready")
        bv_added = sem("bv_added")
        xnT_done = sem("xnT_done")
        xnT_ready = sem("xnT_ready")
        kv_done = sem("kv_done")
        kv_hi_ready = sem("kv_hi_ready")
        q_done = sem("q_done")
        kv_ready = sem("kv_ready")
        qT_ready = sem("qT_ready")
        q_bias_ready = sem("q_bias_ready")
        q_hi_ready = sem("q_hi_ready")
        q_ready = sem("q_ready")
        s_done = sem("s_done")
        max_ready = sem("max_ready")
        p_ready = sem("p_ready")
        pT_done = sem("pT_done")
        pT_hi_ready = sem("pT_hi_ready")
        pT_lo_ready = sem("pT_lo_ready")
        inv_ready = sem("inv_ready")
        pv_done = sem("pv_done")
        x1_ready = sem("x1_ready")
        moments2_ready = sem("moments2_ready")
        rstd2_ready = sem("rstd2_ready")
        xf_ready = sem("xf_ready")
        xfT_done = sem("xfT_done")
        xfT_ready = sem("xfT_ready")
        logits_done = sem("logits_done")
        logit_ready = sem("logit_ready")
        best_ready = sem("best_ready")
        gap_ready = sem("gap_ready")
        gap_exp = sem("gap_exp")
        member_ready = sem("member_ready")
        rank_done = sem("rank_done")
        hot_ready = sem("hot_ready")
        expert_hot_ready = sem("expert_hot_ready")
        started_ready = sem("started_ready")
        experts_ready = sem("experts_ready")
        b1_done = sem("b1_done")
        b1_ready = sem("b1_ready")
        slots_done = sem("slots_done")
        slots_ready = sem("slots_ready")
        token_ready = sem("token_ready")
        xb_ready = sem("xb_ready")
        xT_done = sem("xT_done")
        xT_ready = sem("xT_ready")
        h_done = sem("h_done")
        w2_hi_ready = sem("w2_hi_ready")
        w2_ready = sem("w2_ready")
        h_hi_ready = sem("h_hi_ready")
        h_ready = sem("h_ready")
        z_done = sem("z_done")
        z_read = sem("z_read")
        y_moments = sem("y_moments")
        y_rstd = sem("y_rstd")
        y_ready = sem("y_ready")
        index_ready = sem("index_ready")
        dve_setup = sem("dve_setup")
        moment_step = sem("moment_step")
        softmax_step = sem("softmax_step")
        finish_step = sem("finish_step")
        top_step = sem("top_step")
        route_step = sem("route_step")
        y_step = sem("y_step")
        relu_step = sem("relu_step")
        pool_step = sem("pool_step")

        block = ctx.enter_context(nc.Block())

        PT_PARTS = []
        for b in range(0, T, CHUNKS_PER_BANK):
            whole = min(b + CHUNKS_PER_BANK, T - 1)
            PT_PARTS.append([(b // CHUNKS_PER_BANK, 0, b, whole, P)])
            if b + CHUNKS_PER_BANK >= T:
                PT_PARTS[-1].append((b // CHUNKS_PER_BANK, (T - 1 - b) * P, T - 1, T, TAIL))
        PT_BANKS = len(PT_PARTS)

        def turned(bank, at, a, b, rows):
            return psum[0:rows, 3 + bank, at:at + (b - a) * P]

        def chunks(tensor, a, b, rows):
            return tensor[0:rows, a:b, :].rearrange("p j n -> p (j n)")

        def row(a):
            return a.rearrange("p a d -> p (a d)")

        @block.sync
        def _(sp):
            sp.dma_start(x_res[:, 0, :], x[0:P, :]).then_inc(x0_loaded, 16)
            sp.dma_start(x_res[:, 1:3, :], x[P:3 * P, :].rearrange("(t p) d -> p t d", p=P)).then_inc(x12_loaded, 16)
            sp.dma_start(wqkv[:, 1], wkT.rearrange("(c p) o -> p c o", p=P)).then_inc(w_loaded, 16)
            sp.dma_start(wqkv[:, 2], wvT.rearrange("(c p) o -> p c o", p=P)).then_inc(w_loaded, 16)
            sp.dma_start(wqkv[:, 0], wqT.rearrange("(c p) o -> p c o", p=P)).then_inc(w_loaded, 16)
            sp.dma_start(bias_qk[:], bias_cols).then_inc(small_loaded, 16)
            sp.dma_start(bv_rows[:, :], bv.rearrange("(a d) -> a d", a=1).broadcast_to((P, D)))\
                .then_inc(small_loaded, 16)
            sp.dma_start(router[:, :, :], router_w.rearrange("(c p) e -> p c e", p=P)).then_inc(small_loaded, 16)
            sp.dma_start(x_res[:, 3:T - 1, :], x[3 * P:(T - 1) * P, :].rearrange("(t p) d -> p t d", p=P))\
                .then_inc(x_loaded, 16)
            sp.wait_ge(pad_zeroed, 1)
            sp.dma_start(x_res[0:TAIL, T - 1, :], x[(T - 1) * P:N, :]).then_inc(x_loaded, 16)
            for u in range(2):
                sp.dma_start(adj_sb[:, u, :], adj[u * P:(u + 1) * P, :]).then_inc(adj_loaded[u], 16)
            with sp.Fori(0, E) as e:
                sp.dma_start(w2_sb[:, bass.ds(e, 1)], w2[bass.ds(e, 1)].rearrange("a (c p) d -> p a c d", p=P))\
                    .then_inc(w2_loaded, 16)
            sp.dma_start(norm_sb[:].rearrange("p e a d -> p (e a d)"), norm_rows.rearrange("(o e) a d -> o (e a d)", o=1)
                         .broadcast_to((P, E * 3 * D))).then_inc(norm_loaded, 16)
            sp.wait_ge(q_done, T)
            sp.dma_start(b1_rows[:], b1).then_inc(b1_loaded, 16)

            def store_tile(t, rows):
                sp.wait_ge(x1_ready, t + 1)
                sp.dma_start(sum_dram[bass.ds(t * P, rows), :], row(x_res[0:rows, bass.ds(t, 1), :]))\
                    .then_inc(x1_stored, 16)
                sp.wait_ge(xf_ready, t + 1)
                sp.dma_start(xf_dram[bass.ds(t * P, rows), :], xf_now[0:rows, :]).then_inc(xf_stored, 16)

            def load_adj(t, u, rows):
                sp.wait_ge(p_ready, t - 1)
                sp.dma_start(adj_sb[0:rows, u, :], adj[bass.ds(t * P, rows), :]).then_inc(adj_loaded[u], 16)

            assert T % 2 == 1
            with sp.Fori(0, T - 4, 2) as i:
                for u in range(2):
                    load_adj(i + u + 2, u, P)
                    store_tile(i + u, P)
            load_adj(T - 1, (T - 1) % 2, TAIL)
            sp.dma_start(sum_dram[N:N + P, :], x_res[:, 0, :]).then_inc(x1_stored, 16)
            for t in range(T - 3, T):
                store_tile(t, TAIL if t == T - 1 else P)

            def load_w1(i, u):
                e = sp.value_load(tile_expert_i[0:1, bass.ds(i, 1)], min_val=0, max_val=E - 1)
                sp.dma_start(w1_now[:, u:u + 1], w1[bass.ds(e, 1)].rearrange("a (c p) f -> p a c f", p=P))\
                    .then_inc(w1_loaded[u], 16)

            sp.wait_ge(experts_ready, 1)
            sp.wait_ge(pv_done, T)
            load_w1(0, 0)
            load_w1(1, 1)
            sp.wait_ge(h_done, HB)
            load_w1(2, 0)
            with sp.Fori(2, SLOT_TILES - 2, 2) as i:
                for u in range(2):
                    sp.wait_ge(h_done, HB * (i + u))
                    load_w1(i + u + 1, 1 - u)

            sp.wait_ge(sum_added, 16 * SLOT_TILES)
            sp.dma_start(out, sum_dram[0:N, :]).then_inc(out_stored, 16)
            sp.wait_ge(out_stored, 16)

        @block.tensor
        def _(pe):
            def keep_busy(n):
                for _ in range(n):
                    pe.matmul(psum[:, 7, :], ident[:], ident[:].unsqueeze(1).broadcast_to((P, BANK // P, P)),
                              start=True, stop=True)

            pe.wait_ge(consts, 1)
            keep_busy(2)

            def turn_xn(t):
                pe.wait_ge(xn_ready, t + 1)
                for c in range(DC):
                    m = pe.transpose(psum[:, 0, c * P:(c + 1) * P], xn[:, c * P:(c + 1) * P], ident[:])
                m.then_inc(xnT_done, 1)

            def project(t, u):
                pe.wait_ge(xnT_ready, t + 1)
                for w, bank, done in ((1, 1 + u, kv_done), (0, 3 + u, q_done)):
                    if w == 1:
                        for c in range(DC):
                            pe.matmul(psum[:, bank, D:2 * D], xnT[:, u, c, :], wqkv[:, 2, c, :],
                                      start=(c == 0), stop=(c == DC - 1))
                    for o in range(DC):
                        for c in range(DC):
                            m = pe.matmul(psum[:, bank, o * P:(o + 1) * P], wqkv[:, w, c, o * P:(o + 1) * P],
                                          xnT[:, u, c, :], start=(c == 0), stop=(c == DC - 1))
                    m.then_inc(done, 1)

            turn_xn(0)
            keep_busy(1)
            pe.wait_ge(w_loaded, 48)
            pe.wait_ge(xnT_ready, 1)
            turn_xn(1)
            project(0, 0)
            pe.wait_ge(xnT_ready, 2)
            turn_xn(2)
            project(1, 1)
            with pe.Fori(2, T - 2, 2) as i:
                for u in range(2):
                    t = i + u
                    pe.wait_ge(xnT_ready, t + 1)
                    turn_xn(t + 1)
                    pe.wait_ge(kv_ready, t - 1)
                    pe.wait_ge(qT_ready, t - 1)
                    project(t, u)
            pe.wait_ge(kv_ready, T - 2)
            pe.wait_ge(qT_ready, T - 2)
            project(T - 1, 0)

            def scores(t):
                pe.wait_ge(q_ready, t + 1)
                for b, (k0, kn) in enumerate(KEY_BANKS):
                    for c in range(DC):
                        for j, (q, k) in enumerate(((q_hi, k_hi), (q_hi, k_lo), (q_lo, k_hi))):
                            m = pe.matmul(psum[:, b, 0:kn], q[:, c, :], k[:, c, k0:k0 + kn],
                                          start=(c == 0 and j == 0), stop=(c == DC - 1 and j == 2))
                m.then_inc(s_done, 1)

            def turn_probs(t):
                pe.wait_ge(p_ready, t + 1)
                for j in range(T):
                    rows = min(P, N - j * P)
                    a = j % CHUNKS_PER_BANK * P
                    m = pe.transpose(psum[0:rows, 3 + j // CHUNKS_PER_BANK, a:a + P],
                                     prob[:, j * P:j * P + rows], ident[:])
                m.then_inc(pT_done, 1)

            def weigh(p, v, b, first=False, last=False):
                m = None
                for j in range(b * CHUNKS_PER_BANK, min(T, (b + 1) * CHUNKS_PER_BANK)):
                    rows = min(P, N - j * P)
                    m = pe.matmul(psum[:, 6, 0:D], p[0:rows, j, :], v[0:rows, j, :],
                                  start=(first and j == 0), stop=(last and j == T - 1))
                return m

            def weigh_high(t):
                for b in range(PT_BANKS):
                    pe.wait_ge(pT_hi_ready, PT_BANKS * t + b + 1)
                    weigh(pT_hi, v_hi, b, first=True)
                    weigh(pT_hi, v_lo, b)

            def weigh_low(t):
                for b in range(PT_BANKS):
                    pe.wait_ge(pT_lo_ready, PT_BANKS * t + b + 1)
                    m = weigh(pT_lo, v_hi, b, last=True)
                m.then_inc(pv_done, 1)

            def turn_xf(t):
                pe.wait_ge(xf_ready, t + 1)
                for c in range(DC):
                    m = pe.transpose(psum[:, 7, c * P:(c + 1) * P], xf_now[:, c * P:(c + 1) * P], ident[:])
                m.then_inc(xfT_done, 1)

            def logits(t):
                pe.wait_ge(xfT_ready, t + 1)
                for c in range(DC):
                    m = pe.matmul(psum[:, 7, D:D + E], xfT[:, c, :], router[:, c, :],
                                  start=(c == 0), stop=(c == DC - 1))
                m.then_inc(logits_done, 1)

            pe.wait_ge(kv_ready, T)
            pe.wait_ge(small_loaded, 48)
            scores(0)
            keep_busy(4)
            turn_probs(0)
            scores(1)
            weigh_high(0)
            weigh_low(0)
            turn_probs(1)
            scores(2)
            turn_xf(0)
            weigh_high(1)
            logits(0)
            weigh_low(1)
            with pe.Fori(2, T - 1) as t:
                turn_probs(t)
                scores(t + 1)
                pe.wait_ge(logit_ready, t - 1)
                turn_xf(t - 1)
                weigh_high(t)
                logits(t - 1)
                weigh_low(t)
            turn_probs(T - 1)
            pe.wait_ge(x1_ready, T - 1)
            weigh_high(T - 1)
            weigh_low(T - 1)
            pe.wait_ge(logit_ready, T - 2)
            turn_xf(T - 2)
            logits(T - 2)
            pe.wait_ge(logit_ready, T - 1)
            turn_xf(T - 1)
            logits(T - 1)

            pe.wait_ge(member_ready, 1)
            flat = T * E
            members = member[:].rearrange("p t e -> p (t e)")
            pe.matmul(psum[:, 0, 0:flat], before[:], members, start=True, stop=False)
            for d in range(1, T):
                pe.matmul(psum[:, 0, d * E:flat], ones[:], members[:, 0:flat - d * E], start=False, stop=(d == T - 1))
            for t in range(T):
                rows = TAIL if t == T - 1 else P
                m = pe.matmul(psum[:, 0, flat:flat + E], ones[0:rows, :], member[0:rows, t, :],
                              start=(t == 0), stop=(t == T - 1))
            m.then_inc(rank_done, 1)
            for h, (t0, t1) in enumerate(ROUTE_STEPS):
                pe.wait_ge(hot_ready, h + 1)
                for a in range(t0 * K, t1 * K):
                    rows = TAIL if a // K == T - 1 else P
                    m = pe.matmul(psum[:, 1, 0:PARTS * TELL],
                                  row_hot[0:rows, a, :], blk_hot[0:rows, a].rearrange("p c s -> p (c s)"),
                                  start=(a == 0), stop=(a == TK - 1))
            m.then_inc(slots_done, 1)
            pe.wait_ge(expert_hot_ready, 1)
            pe.wait_ge(b1_loaded, 16)
            for c in range(FC):
                m = pe.matmul(psum[:, 2, c * SLOT_TILES:(c + 1) * SLOT_TILES], b1_rows[:, c * P:(c + 1) * P],
                              expert_hot[:], start=True, stop=True)
            m.then_inc(b1_done, 1)

            def turn_x(i, u):
                pe.wait_ge(x_gathered[u], 8 * (i - u) + 16)
                for c in range(DC):
                    m = pe.transpose(psum[:, 5, c * P:(c + 1) * P], x_slot[:, u, c * P:(c + 1) * P], ident[:])
                m.then_inc(xT_done, 1)

            def layer1(i, u):
                pe.wait_ge(xT_ready, i + 1)
                pe.wait_ge(w1_loaded[u], 8 * (i - u) + 16)
                for b in range(HB):
                    for f in range(CHUNKS_PER_BANK):
                        at = (b * CHUNKS_PER_BANK + f) * P
                        for c in range(DC):
                            m = pe.matmul(psum[:, 2 * u + b, f * P:(f + 1) * P], w1_now[:, u, c, at:at + P],
                                          xT_slot[:, c, :], start=(c == 0), stop=(c == DC - 1))
                    m.then_inc(h_done, 1)

            def layer2(i, u):
                pe.wait_ge(w2_ready, i + 1)
                pe.wait_ge(h_ready, HB * i + HB)
                for c in range(FC):
                    for j, (h, w) in enumerate(((h_hi, w2_hi), (h_hi, w2_lo), (h_lo, w2_hi))):
                        m = pe.matmul(psum[:, 4 + 2 * u, 0:D], h[u][:, c, :], w[u][:, c, :],
                                      start=(c == 0 and j == 0), stop=(c == FC - 1 and j == 2))
                m.then_inc(z_done, 1)

            pe.wait_ge(slots_ready, 2)
            turn_x(0, 0)
            keep_busy(1)
            layer1(0, 0)
            turn_x(1, 1)
            pe.wait_ge(b1_ready, 1)
            layer1(1, 1)
            turn_x(2, 0)
            layer2(0, 0)
            with pe.Fori(2, SLOT_TILES - 2, 2) as i:
                for u in range(2):
                    layer1(i + u, u)
                    turn_x(i + u + 1, 1 - u)
                    layer2(i + u - 1, 1 - u)
            last = SLOT_TILES - 1
            layer1(last, 0)
            layer2(last - 1, 1)
            layer2(last, 0)

        @block.vector
        def _(dve):
            def hold():
                dve.memset(held_dve[:], 0.0)

            dve.memset(x_res[64:P, T - 1, :], 0.0).then_inc(pad_zeroed, 1)
            dve.memset(minus_half[:], -0.5).then_inc(dve_setup, 1)
            dve.memset(zero_eps[:, 0:1], 0.0)
            dve.memset(zero_eps[:, 1:2], LN_EPS)
            dve.wait_ge(iotas, 1)
            dve.tensor_scalar(ident[:], col[:], part[:, 0:1], None, ALU.is_equal).then_inc(consts, 1)

            def find_moments(t):
                dve.bn_stats(stats[:], row(x_res[:, bass.ds(t, 1), :])).then_inc(moment_step, 1)
                dve.wait_ge(moment_step, 2 * t + 1)
                hold()
                dve.bn_aggr(moments[:], stats[:]).then_inc(moment_step, 1)
                dve.wait_ge(moment_step, 2 * t + 2)
                dve.scalar_tensor_tensor(mean_var[:, bass.ds(t, 1), :], moments[:].unsqueeze(1), 1.0, zero_eps[:].unsqueeze(1),
                                         ALU.mult, ALU.add).then_inc(moments_ready, 1)

            def normalise(t):
                dve.wait_ge(rstd_ready, t + 1)
                dve.tensor_scalar(xn[:], row(x_res[:, bass.ds(t, 1), :]), row(mean_var[:, bass.ds(t, 1), 0:1]),
                                  rstd[:, bass.ds(t, 1)], ALU.subtract, ALU.mult).then_inc(xn_ready, 1)

            def take_kv(t, u):
                kv = psum[:, 1 + u:2 + u, :]
                dve.wait_ge(kv_hi_ready, t + 1)
                for o in range(DC):
                    at = bass.ds(t * P, P)
                    dve.scalar_tensor_tensor(k_lo[:, o, at], row(kv[:, :, o * P:(o + 1) * P]), bias_qk[:, 1, o:o + 1],
                                             k_hi[:, o, at].bitcast(F32), ALU.add, ALU.subtract)
                m = dve.scalar_tensor_tensor(v_lo[:, bass.ds(t, 1), :], kv[:, :, D:2 * D], 1.0,
                                         v_hi[:, bass.ds(t, 1), :].bitcast(F32), ALU.mult, ALU.subtract)
                m.then_inc(kv_ready, 1)

            def take_q(t):
                dve.wait_ge(q_hi_ready, t + 1)
                dve.scalar_tensor_tensor(q_lo[:], qT[:, :, bass.ds(t * P, P)], 1.0, q_hi[:].bitcast(F32),
                                         ALU.mult, ALU.subtract).then_inc(q_ready, 1)

            dve.wait_ge(x0_loaded, 16)
            find_moments(0)
            normalise(0)
            dve.wait_ge(x12_loaded, 16)
            find_moments(1)
            find_moments(2)
            dve.wait_ge(xnT_done, 1)
            normalise(1)
            dve.wait_ge(small_loaded, 48)
            dve.tensor_scalar(q_bias[:], bias_qk[:, 0], QK_SCALE, None, ALU.mult).then_inc(q_bias_ready, 1)
            dve.wait_ge(xnT_done, 2)
            normalise(2)
            dve.wait_ge(x_loaded, 32)
            find_moments(3)
            find_moments(4)
            with dve.Fori(1, T - 5, 2) as i:
                for u in range(2):
                    dve.wait_ge(xnT_done, i + u + 2)
                    normalise(i + u + 2)
                    take_kv(i + u - 1, u)
                    find_moments(i + u + 4)
            for t in range(T - 4, T + 1):
                if t < T - 2:
                    dve.wait_ge(xnT_done, t + 2)
                    normalise(t + 2)
                take_kv(t - 1, (t - 1) % 2)
                if t == T - 1:
                    take_q(0)

            dve.wait_ge(q_done, T)
            dve.memset(ones[:], 1.0)
            dve.tensor_scalar(before[:], col[:], part[:, 0:1], None, ALU.is_gt)

            def take_scores(t, u):
                dve.wait_ge(adj_loaded[u], 8 * (t - u) + 16)
                dve.wait_ge(s_done, t + 1)
                hold()
                dve.tensor_tensor_reduce(adj_sb[:, u, :], psum[:, 0:len(KEY_BANKS), :]
                                         .rearrange("p b n -> p (b n)")[:, 0:N], adj_sb[:, u, :], 2.0, LEAST,
                                         ALU.add, ALU.max, row_max[:]).then_inc(softmax_step, 1)
                dve.wait_ge(softmax_step, t + 1)
                dve.tensor_scalar(neg_max[:], row_max[:], -1.0, None, ALU.mult).then_inc(max_ready, 1)

            def take_probs(t):
                for b, parts in enumerate(PT_PARTS):
                    dve.wait_ge(pT_hi_ready, PT_BANKS * t + b + 1)
                    for bank, at, c0, c1, rows in parts:
                        m = dve.tensor_tensor(chunks(pT_lo, c0, c1, rows), turned(bank, at, c0, c1, rows),
                                              chunks(pT_hi, c0, c1, rows).bitcast(F32), ALU.subtract)
                    m.then_inc(pT_lo_ready, 1)
                dve.reciprocal(row_inv[:], row_sum[:]).then_inc(inv_ready, 1)

            def take_logit(t):
                dve.wait_ge(logits_done, t + 1)
                hold()
                dve.max(top[:], psum[:, 7, D:D + E]).then_inc(top_step, 1)
                dve.wait_ge(top_step, t + 1)
                hold()
                dve.max_index(top_at[:], top[:], psum[:, 7, D:D + E]).then_inc(logit_ready, 1)
                dve.wait_ge(logit_ready, t + 1)
                dve.tensor_scalar(best[:, bass.ds(t, 1), :], top[:, 0:K].unsqueeze(1), 1.0, None, ALU.mult)
                dve.tensor_scalar(best_at[:, bass.ds(t, 1), :], top_at[:, 0:K].unsqueeze(1), 1.0, None, ALU.mult)\
                    .then_inc(best_ready, 1)

            def add_attention(t):
                xt = row(x_res[:, bass.ds(t, 1), :])
                dve.wait_ge(pv_done, t + 1)
                dve.wait_ge(inv_ready, t + 1)
                dve.scalar_tensor_tensor(xt, psum[:, 6, 0:D], row_inv[:, 0:1], xt, ALU.mult, ALU.add)\
                    .then_inc(x1_ready, 1)
                dve.wait_ge(x1_ready, t + 1)
                hold()
                dve.bn_stats(stats2[:], xt).then_inc(finish_step, 1)
                dve.wait_ge(finish_step, 2 * t + 1)
                hold()
                dve.bn_aggr(moments2[:], stats2[:]).then_inc(finish_step, 1)
                dve.wait_ge(finish_step, 2 * t + 2)
                dve.tensor_scalar(var2[:], moments2[:, 1:2], LN_EPS, None, ALU.add).then_inc(moments2_ready, 1)

            def norm_x(t, first=False):
                if not first:
                    dve.wait_ge(xfT_done, t)
                    dve.wait_ge(xf_stored, 16 * t)
                dve.wait_ge(rstd2_ready, t + 1)
                dve.tensor_scalar(xf_now[:], row(x_res[:, bass.ds(t, 1), :]), moments2[:, 0:1], rstd2[:, 0:1],
                                  ALU.subtract, ALU.mult).then_inc(xf_ready, 1)

            def attend(t, u, first=False):
                add_attention(t - 1)
                take_probs(t)
                norm_x(t - 1, first)
                take_scores(t + 1, 1 - u)

            dve.wait_ge(bv_added, T)
            take_scores(0, 0)
            take_q(1)
            take_probs(0)
            take_scores(1, 1)
            take_q(2)
            attend(1, 1, first=True)
            take_q(3)
            take_logit(0)
            with dve.Fori(2, T - 4, 2) as i:
                for u in range(2):
                    attend(i + u, u)
                    take_q(i + u + 2)
                    take_logit(i + u - 1)
            attend(T - 3, 0)
            take_q(T - 1)
            take_logit(T - 4)
            attend(T - 2, 1)
            take_logit(T - 3)
            add_attention(T - 2)
            take_probs(T - 1)
            norm_x(T - 2)
            add_attention(T - 1)
            take_logit(T - 2)
            norm_x(T - 1)
            take_logit(T - 1)

            steps = [0]

            def link(ins):
                steps[0] += 1
                ins.then_inc(route_step, 1)
                dve.wait_ge(route_step, steps[0])

            dve.wait_ge(best_ready, T)
            dve.wait_ge(routing_consts, 1)
            link(dve.tensor_tensor(hot[:].rearrange("p t k e -> p (t k) e"),
                                   expert_no[:].unsqueeze(1).broadcast_to((P, TK, E)),
                                   best_at[:].rearrange("p t k -> p (t k)").unsqueeze(2).broadcast_to((P, TK, E)),
                                   ALU.is_equal))
            dve.tensor_tensor(member[:], hot[:, :, 0, :], hot[:, :, 1, :], ALU.add).then_inc(member_ready, 1)
            dve.tensor_tensor(gate_tmp[:, 0], best[:, :, 1], best[:, :, 0], ALU.subtract).then_inc(gap_ready, 1)
            dve.wait_ge(gap_exp, 1)
            link(dve.tensor_scalar(gate_tmp[:, 2], gate_tmp[:, 1], 1.0, None, ALU.add))
            link(dve.reciprocal(gates[:, :, 0], gate_tmp[:, 2]))
            link(dve.tensor_tensor(gates[:, :, 1], gate_tmp[:, 1], gates[:, :, 0], ALU.mult))
            gate_flat = gates[:].rearrange("p t k -> p (t k)")
            dve.tensor_copy(told[:, :, 1], gate_flat)
            link(dve.tensor_copy(gate_hi[:], gate_flat))
            dve.tensor_tensor(told[:, :, 2], gate_flat, gate_hi[:].bitcast(F32), ALU.subtract)
            dve.wait_ge(rank_done, 1)
            counts = psum[:, 0, T * E:T * E + E].unsqueeze(2).broadcast_to((P, E, T))
            link(dve.tensor_tensor(tile_cmp[:], counts, tile_edges[:].unsqueeze(1).broadcast_to((P, E, T)), ALU.is_gt))
            link(dve.tensor_reduce(tiles_of[:], tile_cmp[:], AX.X, ALU.add))
            link(dve.tensor_tensor(start_cmp[:], lower[:], tiles_of[:].unsqueeze(1).broadcast_to((P, E, E)), ALU.mult))
            link(dve.tensor_reduce(block_start[:], start_cmp[:], AX.X, ALU.add))
            dve.tensor_tensor(expert_cmp[:], tile_no[:, 0:SLOT_TILES].unsqueeze(2).broadcast_to((P, SLOT_TILES, E)),
                              block_start[:].unsqueeze(1).broadcast_to((P, SLOT_TILES, E)), ALU.is_ge)\
                .then_inc(started_ready, 1)
            link(dve.scalar_tensor_tensor(slot_base[:], block_start[:].unsqueeze(1).broadcast_to((P, T, E)), float(P),
                                          psum[:, 0, 0:T * E].rearrange("p (t e) -> p t e", e=E),
                                          ALU.mult, ALU.add))
            for k in range(K):
                m = dve.tensor_tensor(slot_pick[:].rearrange("p (t k) e -> p t k e", k=K)[:, :, k, :],
                                      hot[:, :, k, :], slot_base[:], ALU.mult)
            link(m)
            link(dve.tensor_reduce(slot_f[:], slot_pick[:], AX.X, ALU.add))
            link(dve.tensor_copy(slot_i[:], slot_f[:]))
            dve.tensor_scalar(slot_low_i[:], slot_i[:], P - 1, None, ALU.bitwise_and)
            link(dve.tensor_scalar(slot_blk_i[:], slot_i[:], P.bit_length() - 1, None, ALU.logical_shift_right))
            dve.tensor_copy(slot_low[:], slot_low_i[:])
            link(dve.tensor_copy(slot_blk[:], slot_blk_i[:]))
            for t0, t1 in ROUTE_STEPS:
                a0, a1 = t0 * K, t1 * K
                shape = (P, a1 - a0, TELL)
                link(dve.tensor_tensor(blk_is[:, a0:a1], tile_no[:].unsqueeze(1).broadcast_to(shape),
                                       slot_blk[:, a0:a1].unsqueeze(2).broadcast_to(shape), ALU.is_equal))
                shape = (P, a1 - a0, PARTS, TELL)
                dve.tensor_tensor(blk_hot[:, a0:a1], blk_is[:, a0:a1].unsqueeze(2).broadcast_to(shape),
                                  told[:, a0:a1].unsqueeze(3).broadcast_to(shape), ALU.mult)
                dve.tensor_tensor(row_hot[:, a0:a1], col[:].unsqueeze(1).broadcast_to((P, a1 - a0, P)),
                                  slot_low[:, a0:a1].unsqueeze(2).broadcast_to((P, a1 - a0, P)), ALU.is_equal)\
                    .then_inc(hot_ready, 1)
            dve.wait_ge(slots_done, 1)
            found = psum[:, 1, 0:SLOT_TILES]
            dve.tensor_scalar(slot_token[:], found, -1.0, 0.0, ALU.add, ALU.max).then_inc(slots_ready, 1)
            link(dve.tensor_scalar(slot_tmp[:], found, 0.0, spare[:, 0:1], ALU.is_equal, ALU.mult))
            dve.scalar_tensor_tensor(slot_row[:], found, -1.0, slot_tmp[:], ALU.add, ALU.max)
            dve.tensor_reduce(slot_gate[:], psum[:, 1, TELL:3 * TELL].rearrange("p (c s) -> p s c", c=2)
                              [:, 0:SLOT_TILES, :], AX.X, ALU.add).then_inc(slots_ready, 1)

            def expert_of(i):
                return dve.value_load(tile_expert_i[0:1, bass.ds(i, 1)], min_val=0, max_val=E - 1)

            def find_y_moments(i, u, e):
                dve.wait_ge(xb_ready, i + 1)
                dve.wait_ge(z_done, i + 1)
                dve.tensor_tensor(y_sum[:], psum[:, 4 + 2 * u, 0:D], row(xb_slot[:, bass.ds(i % XB_RING, 1), :]), ALU.add)\
                    .then_inc(z_read, 1)
                dve.wait_ge(z_read, i + 1)
                dve.bn_stats(stats2[:], y_sum[:]).then_inc(y_step, 1)
                dve.wait_ge(y_step, 4 * i + 1)
                hold()
                dve.bn_aggr(moments2[:], stats2[:]).then_inc(y_step, 1)
                dve.wait_ge(y_step, 4 * i + 2)
                dve.tensor_scalar(var2[:], moments2[:, 1:2], EXPERT_EPS, None, ALU.add).then_inc(y_moments, 1)
                dve.scalar_tensor_tensor(y_mid[:], y_sum[:], moments2[:, 0:1],
                                         row(norm_sb[:, bass.ds(e, 1), 1, :]),
                                         ALU.subtract, ALU.mult).then_inc(y_step, 1)

            def finish_y(i, u, e):
                dve.wait_ge(y_step, 4 * i + 3)
                dve.wait_ge(y_rstd, i + 1)
                dve.scalar_tensor_tensor(y_mid[:], y_mid[:], rstd2[:, 0:1],
                                         row(norm_sb[:, bass.ds(e, 1), 2, :]),
                                         ALU.mult, ALU.add).then_inc(y_step, 1)
                dve.wait_ge(y_step, 4 * i + 4)
                dve.tensor_scalar(y_out[:, u], y_mid[:], slot_gate[:, bass.ds(i, 1)], None, ALU.mult)\
                    .then_inc(y_ready, 1)

            dve.wait_ge(b1_done, 1)
            dve.tensor_copy(b1_tiles[:].rearrange("p i c -> p c i"),
                            psum[:, 2, 0:FC * SLOT_TILES].rearrange("p (c i) -> p c i", c=FC)).then_inc(b1_ready, 1)

            def split_w2(i, u, e, b):
                if b == 0:
                    dve.wait_ge(w2_hi_ready, i + 1)
                cs = slice(b * CHUNKS_PER_BANK, (b + 1) * CHUNKS_PER_BANK)
                m = dve.tensor_tensor(w2_lo[u][:, cs, :].rearrange("p c d -> p (c d)"),
                                      w2_sb[:, bass.ds(e, 1), cs, :].rearrange("p e c d -> p (e c d)"),
                                      w2_hi[u][:, cs, :].rearrange("p c d -> p (c d)").bitcast(F32), ALU.subtract)
                if b == HB - 1:
                    m.then_inc(w2_ready, 1)

            def split_h(i, u, b):
                dve.wait_ge(h_hi_ready, HB * i + b + 1)
                at = slice(b * BANK, (b + 1) * BANK)
                dve.tensor_tensor(h_lo[u][:].rearrange("p c n -> p (c n)")[:, at], hT_sb[:, at],
                                  h_hi[u][:].rearrange("p c n -> p (c n)")[:, at].bitcast(F32), ALU.subtract)\
                    .then_inc(h_ready, 1)

            def step(i, u, finish=True, first=False, last=False):
                e = expert_of(i)
                if finish:
                    e_before = expert_of(i - 2)
                    find_y_moments(i - 2, u, e_before)
                split_w2(i, u, e, 0)
                if finish and not last:
                    if not first:
                        dve.wait_ge(sum_added, 16 * i - 48)
                    finish_y(i - 2, u, e_before)
                split_h(i, u, 0)
                split_w2(i, u, e, 1)
                split_h(i, u, 1)
                if last:
                    dve.wait_ge(sum_added, 16 * i - 48)
                    finish_y(i - 2, u, e_before)

            dve.wait_ge(norm_loaded, 16)
            dve.wait_ge(experts_ready, 1)
            step(0, 0, finish=False)
            step(1, 1, finish=False)
            step(2, 0, first=True)
            step(3, 1, first=True)
            with dve.Fori(4, SLOT_TILES - 2, 2) as i:
                step(i, 0)
                step(i + 1, 1)
            last = SLOT_TILES - 1
            step(last, 0, last=True)
            for i in (last - 1, last):
                e = expert_of(i)
                find_y_moments(i, i % 2, e)
                dve.wait_ge(sum_added, 16 * (i - 1))
                finish_y(i, i % 2, e)

        @block.scalar
        def _(act):
            def take_xnT(t, u):
                act.wait_ge(xnT_done, t + 1)
                act.activation(xnT[:, u].rearrange("p c n -> p (c n)"), psum[:, 0, 0:D], ACT.Copy)\
                    .then_inc(xnT_ready, 1)

            def take_kv(t, u):
                act.wait_ge(kv_done, t + 1)
                act.activation(v_hi[:, bass.ds(t, 1), :], psum[:, 1 + u:2 + u, D:2 * D], ACT.Copy)
                for o in range(DC):
                    m = act.activation(k_hi[:, o, bass.ds(t * P, P)], psum[:, 1 + u, o * P:(o + 1) * P],
                                       ACT.Identity, bias=bias_qk[:, 1, o:o + 1])
                m.then_inc(kv_hi_ready, 1)

            def take_queries(t, u):
                act.wait_ge(q_done, t + 1)
                for o in range(DC):
                    m = act.activation(qT[:, o, bass.ds(t * P, P)], psum[:, 3 + u, o * P:(o + 1) * P],
                                       ACT.Identity, bias=q_bias[:, o:o + 1], scale=QK_SCALE)
                m.then_inc(qT_ready, 1)

            take_xnT(0, 0)
            take_xnT(1, 1)
            act.wait_ge(small_loaded, 48)
            act.wait_ge(q_bias_ready, 1)
            with act.Fori(0, T - 4, 2) as i:
                for u in range(2):
                    take_kv(i + u, u)
                    act.wait_ge(q_done, i + u + 1)
                    take_xnT(i + u + 2, u)
                    take_queries(i + u, u)
            take_kv(T - 3, 0)
            act.wait_ge(q_done, T - 2)
            take_xnT(T - 1, 0)
            take_queries(T - 3, 0)
            take_kv(T - 2, 1)
            act.wait_ge(qT_ready, 1)
            act.activation(q_hi[:], qT[:, :, 0:P], ACT.Copy).then_inc(q_hi_ready, 1)
            take_queries(T - 2, 1)
            take_kv(T - 1, 0)
            take_queries(T - 1, 0)

            def take_q(t):
                act.activation(q_hi[:], qT[:, :, bass.ds(t * P, P)], ACT.Copy).then_inc(q_hi_ready, 1)

            def exponentials(t, u):
                act.wait_ge(max_ready, t + 1)
                act.activation(prob[:], adj_sb[:, u, :], ACT.Exp, bias=neg_max[:, 0:1], accum_out=row_sum[:, 0:1])\
                    .then_inc(p_ready, 1)

            def take_probs(t):
                act.wait_ge(pT_done, t + 1)
                for parts in PT_PARTS:
                    for bank, at, c0, c1, rows in parts:
                        m = act.activation(chunks(pT_hi, c0, c1, rows), turned(bank, at, c0, c1, rows), ACT.Copy)
                    m.then_inc(pT_hi_ready, 1)

            def take_xfT(t):
                act.wait_ge(xfT_done, t + 1)
                act.activation(xfT[:].rearrange("p c n -> p (c n)"), psum[:, 7, 0:D], ACT.Copy)\
                    .then_inc(xfT_ready, 1)

            def attend(t, u, next_q=True):
                take_probs(t)
                if next_q:
                    act.wait_ge(s_done, t + 2)
                    take_q(t + 2)
                take_xfT(t - 1)
                act.wait_ge(inv_ready, t + 1)
                exponentials(t + 1, 1 - u)

            act.wait_ge(qT_ready, T)
            act.wait_ge(s_done, 1)
            take_q(1)
            exponentials(0, 0)
            take_probs(0)
            act.wait_ge(s_done, 2)
            take_q(2)
            act.wait_ge(inv_ready, 1)
            exponentials(1, 1)
            with act.Fori(1, T - 3, 2) as i:
                attend(i, 1)
                attend(i + 1, 0)
            attend(T - 2, 1, next_q=False)
            take_probs(T - 1)
            take_xfT(T - 2)
            take_xfT(T - 1)

            act.wait_ge(gap_ready, 1)
            act.activation(gate_tmp[:, 1], gate_tmp[:, 0], ACT.Exp).then_inc(gap_exp, 1)

            act.wait_ge(experts_ready, 1)
            act.wait_ge(pv_done, T)
            act.wait_ge(w2_loaded, 16 * E)

            def expert_of(i):
                return act.value_load(tile_expert_i[0:1, bass.ds(i, 1)], min_val=0, max_val=E - 1)

            def split_w2(i, u):
                e = expert_of(i)
                act.activation(w2_hi[u][:], w2_sb[:, bass.ds(e, 1)].rearrange("p e c d -> p (e c) d"), ACT.Copy)\
                    .then_inc(w2_hi_ready, 1)

            def take_xT(i):
                act.wait_ge(xT_done, i + 1)
                act.activation(xT_slot[:].rearrange("p c n -> p (c n)"), psum[:, 5, 0:D], ACT.Copy)\
                    .then_inc(xT_ready, 1)

            def take_h(i, u, b):
                act.wait_ge(h_done, HB * i + b + 1)
                bias = row(b1_tiles[:, bass.ds(i, 1), :])
                for f in range(CHUNKS_PER_BANK):
                    c = b * CHUNKS_PER_BANK + f
                    m = act.activation(hT_sb[:, c * P:(c + 1) * P], psum[:, 2 * u + b, f * P:(f + 1) * P],
                                       ACT.Relu, bias=bias[:, c:c + 1])
                m.then_inc(relu_step, 1)

            def split_h(i, u, b):
                act.wait_ge(relu_step, HB * i + b + 1)
                at = slice(b * BANK, (b + 1) * BANK)
                act.activation(h_hi[u][:].rearrange("p c n -> p (c n)")[:, at], hT_sb[:, at], ACT.Copy)\
                    .then_inc(h_hi_ready, 1)

            def step(i, u, first=False, last=False):
                if not (first and i < 2):
                    act.wait_ge(z_done, i - 1)
                if not (first and i == 0):
                    split_w2(i, u)
                    act.wait_ge(h_ready, HB * i)
                take_h(i, u, 0)
                split_h(i, u, 0)
                if first:
                    take_xT(i + 1)
                take_h(i, u, 1)
                if not (first or last):
                    take_xT(i + 1)
                split_h(i, u, 1)

            assert HB == 2 and SLOT_TILES % 2 == 1
            split_w2(0, 0)
            act.wait_ge(slots_ready, 2)
            take_xT(0)
            act.wait_ge(b1_ready, 1)
            step(0, 0, first=True)
            step(1, 1, first=True)
            with act.Fori(2, SLOT_TILES - 2, 2) as i:
                step(i, 0)
                step(i + 1, 1)
            step(SLOT_TILES - 1, 0, last=True)

        @block.gpsimd
        def _(pool):
            def hold():
                pool.tensor_tensor(held_pool[:], minus_half[:, 0:1], minus_half[:, 0:1], ALU.mult)

            def iota(tensor, pattern, base, per_partition):
                return pool.iota(tensor[:], pattern, base=base, channel_multiplier=per_partition,
                                 allow_small_or_imprecise_dtypes=True)

            iota(col, [[1, P]], 0, 0)
            iota(part, [[1, 1]], 0, 1).then_inc(iotas, 1)
            pool.wait_ge(dve_setup, 1)

            with pool.Fori(0, T) as t:
                pool.wait_ge(moments_ready, t + 1)
                pool.tensor_tensor(rstd[:, bass.ds(t, 1)], row(mean_var[:, bass.ds(t, 1), 1:2]), minus_half[:, bass.ds(t, 1)],
                                   ALU.pow).then_inc(rstd_ready, 1)
            pool.iota(told[:].rearrange("p (t k) c -> p t k c", k=K)[:, :, :, 0], [[P, T], [0, K]], base=1,
                      channel_multiplier=1, allow_small_or_imprecise_dtypes=True)
            iota(spare, [[1, 1]], N, 1)
            iota(tile_no, [[1, TELL]], 0, 0)
            iota(tile_edges, [[P, T]], 0, 0)
            iota(expert_no, [[1, E]], 0, 0)
            iota(order, [[1, E], [-1, E]], 0, 0).then_inc(pool_step, 1)
            pool.wait_ge(pool_step, 1)
            pool.tensor_scalar(lower[:], order[:], 0.0, None, ALU.is_gt).then_inc(routing_consts, 1)

            pool.wait_ge(small_loaded, 48)
            with pool.Fori(0, T) as t:
                pool.wait_ge(xn_ready, t + 1)
                pool.tensor_tensor(x_res[:, bass.ds(t, 1), :], x_res[:, bass.ds(t, 1), :],
                                   bv_rows[:].unsqueeze(1), ALU.add).then_inc(bv_added, 1)

            def rsqrt(t, ready, done):
                pool.wait_ge(ready, t + 1)
                pool.tensor_tensor(rstd2[:], var2[:], minus_half[:, 0:1], ALU.pow).then_inc(done, 1)

            with pool.Fori(0, T) as t:
                rsqrt(t, moments2_ready, rstd2_ready)

            steps = [1]

            def link(ins):
                steps[0] += 1
                ins.then_inc(pool_step, 1)
                pool.wait_ge(pool_step, steps[0])

            assert E == 8
            pool.wait_ge(started_ready, 1)
            for n in (4, 2, 1):
                link(pool.tensor_tensor(expert_cmp[:, :, 0:n], expert_cmp[:, :, 0:n], expert_cmp[:, :, n:2 * n],
                                        ALU.add))
            count = expert_cmp[:, :, 0:1].rearrange("p i e -> p (i e)")
            pool.tensor_scalar(tile_expert_i[:], count, -1.0, None, ALU.add).then_inc(experts_ready, 1)
            pool.tensor_scalar(expert_hot[:], count[0:E], -1.0, part[0:E, 0:1], ALU.add, ALU.is_equal)\
                .then_inc(expert_hot_ready, 1)

            def gather(i, u, first=False):
                tokens = slot_token[:, i:i + 1] if first else token_now[u][:, 0:1]
                if not first:
                    pool.tensor_copy(token_now[u][:], slot_token[:, bass.ds(i, 1)]).then_inc(token_ready, 1)
                    pool.wait_ge(token_ready, i - 1)
                    hold()
                pool.indirect_dma_start(x_slot[:, u], None, xf_dram, bass.IndirectOffsetOnAxis(ap=tokens, axis=0))\
                    .then_inc(x_gathered[u], 16)

            def add_bias(i, u):
                e = pool.value_load(tile_expert_i[0:1, bass.ds(i, 1)], min_val=0, max_val=E - 1)
                pool.wait_ge(xT_done, i + 1)
                pool.tensor_tensor(xb_slot[:, bass.ds(i % XB_RING, 1), :], x_slot[:, u:u + 1],
                                   norm_sb[:, bass.ds(e, 1), 0, :], ALU.add).then_inc(xb_ready, 1)
                pool.wait_ge(xb_ready, i + 1)

            def add_rows(i, u, first=False):
                pool.tensor_copy(row_now[u][:], slot_row[:, bass.ds(i, 1)]).then_inc(index_ready, 1)
                if not first:
                    pool.wait_ge(sum_added, 16 * i)
                pool.wait_ge(index_ready, i + 1)
                pool.wait_ge(y_ready, i + 1)
                hold()
                pool.indirect_dma_start(sum_dram, bass.IndirectOffsetOnAxis(ap=row_now[u][:, 0:1], axis=0),
                                        y_out[:, u], None, compute_op=ALU.add).then_inc(sum_added, 16)

            def step(i, u, prefetch=True, first=False):
                rsqrt(i - 2, y_moments, y_rstd)
                add_bias(i + 1, 1 - u)
                if prefetch:
                    gather(i + 3, 1 - u)
                add_rows(i - 2, u, first)

            pool.wait_ge(xf_stored, 16 * T)
            pool.wait_ge(x1_stored, 16 * (T + 1))
            pool.wait_ge(norm_loaded, 16)
            pool.wait_ge(experts_ready, 1)
            pool.wait_ge(slots_ready, 1)
            gather(0, 0, first=True)
            gather(1, 1, first=True)
            for i in range(3):
                add_bias(i, i % 2)
                gather(i + 2, i % 2)
            pool.wait_ge(slots_ready, 2)
            step(2, 0, first=True)
            step(3, 1)
            with pool.Fori(4, SLOT_TILES - 4, 2) as i:
                step(i, 0)
                step(i + 1, 1)
            last = SLOT_TILES - 1
            for i in range(last - 2, last):
                step(i, i % 2, prefetch=False)
            for i in range(last - 2, SLOT_TILES):
                rsqrt(i, y_moments, y_rstd)
                add_rows(i, i % 2)


_INS = ["x", "adj", "wqT", "wkT", "wvT", "bias_cols", "bv", "router_w", "w1", "b1", "w2", "norm_rows"]


def kernel(x, adj, L0_gnn_Wq, L0_gnn_bq, L0_gnn_Wk, L0_gnn_bk, L0_gnn_Wv, L0_gnn_bv, L0_ffn_router_w, L0_ffn_w1,
           L0_ffn_b1, L0_ffn_w2, L0_ffn_b2, L0_ffn_gamma, L0_ffn_beta):
    import concourse.bacc as bacc
    from concourse.bass_utils import run_bass_kernel_spmd

    rows = [np.asarray(a) for a in (L0_ffn_b2, L0_ffn_gamma, L0_ffn_beta)]
    given = dict(x=x, adj=adj, wqT=np.asarray(L0_gnn_Wq).T, wkT=np.asarray(L0_gnn_Wk).T, wvT=np.asarray(L0_gnn_Wv).T,
                 bias_cols=np.stack([L0_gnn_bq, L0_gnn_bk]).reshape(2, -1, P).transpose(2, 0, 1), bv=L0_gnn_bv,
                 router_w=L0_ffn_router_w, w1=L0_ffn_w1, b1=L0_ffn_b1, w2=L0_ffn_w2, norm_rows=np.stack(rows, axis=1))
    nc = bacc.Bacc("TRN2", target_bir_lowering=False, num_devices=1)
    arrays, args = {}, []
    for name in _INS:
        a = np.ascontiguousarray(given[name])
        arrays[name] = a
        args.append(nc.dram_tensor(name, a.shape, mybir.dt.from_np(a.dtype), kind="ExternalInput").ap())
    out = nc.dram_tensor("out", arrays["x"].shape, F32, kind="ExternalOutput").ap()
    block_kernel(nc, *args, out)
    r = run_bass_kernel_spmd(nc, [arrays], core_ids=[0])
    return r.results[0]["out"]
```
